# Optimizing a Trainium2 kernel written in Bass

```python
import numpy as np
import jax
import jax.numpy as jnp

def _softmax(x, axis=-1):
    return jax.nn.softmax(x, axis=axis)
def _gelu(x):
    return jax.nn.gelu(x, approximate=True)
def _silu(x):
    return jax.nn.silu(x)
def _sigmoid(x):
    return jax.nn.sigmoid(x)
def _layernorm(x, axis=-1, eps=1e-5):
    m = jnp.mean(x, axis=axis, keepdims=True)
    v = jnp.var(x, axis=axis, keepdims=True)
    return (x - m) / jnp.sqrt(v + eps)
def _scatter_add(tgt, idx, src, axis=0):
    return tgt.at[idx].add(src)
def _segment_sum(src, seg, n):
    return jax.ops.segment_sum(src, seg, n)

kernel_name = 'mk_conv_seq_d2_conv_nchw64_35618b'

def setup_inputs(seed: int = 0):
    np.random.seed(seed)
    _w = jnp.asarray
    def _rec_inputs():
        import jax
        import jax.numpy as jnp
        _gk = jax.random.key(seed)
        x = -0.000125 + 0.9999 * jax.random.normal(jax.random.fold_in(_gk, 1), (32, 64, 128, 128), jnp.float32)
        return x
    x = _rec_inputs()
    def _L0_conv_setup():
        import jax, jax.numpy as jnp
        import numpy as np
        NUM_HEADS = 8
        HEAD_DIM = 8
        C_IN = 64
        C_OUT = 64
        EPS = 1e-05

        def _layernorm(x, g, b):
            m = jnp.mean(x, axis=-1, keepdims=True)
            v = jnp.mean((x - m) ** 2, axis=-1, keepdims=True)
            return (x - m) / jnp.sqrt(v + EPS) * g + b
        key = jax.random.key(seed)
        ks = jax.random.split(key, 8)
        B, H, W = (32, 128, 128)
        x = jax.random.normal(ks[0], (B, C_IN, H, W), dtype=jnp.float32)
        W_Q = jax.random.uniform(ks[1], (NUM_HEADS, C_IN, HEAD_DIM), minval=-0.1, maxval=0.1, dtype=jnp.float32)
        W_K = jax.random.uniform(ks[2], (NUM_HEADS, C_IN, HEAD_DIM), minval=-0.1, maxval=0.1, dtype=jnp.float32)
        W_V = jax.random.uniform(ks[3], (NUM_HEADS, C_IN, HEAD_DIM), minval=-0.1, maxval=0.1, dtype=jnp.float32)
        lim = float(np.sqrt(6.0 / (C_IN + C_IN)))
        W_O = jax.random.uniform(ks[4], (NUM_HEADS * HEAD_DIM, C_IN), minval=-lim, maxval=lim, dtype=jnp.float32)
        lw = 1.0 / np.sqrt(C_IN)
        ffn1_w = jax.random.uniform(ks[5], (C_OUT, C_IN), minval=-lw, maxval=lw, dtype=jnp.float32)
        ffn1_b = jnp.zeros((C_OUT,), jnp.float32)
        lw2 = 1.0 / np.sqrt(C_OUT)
        ffn2_w = jax.random.uniform(ks[6], (C_OUT, C_OUT), minval=-lw2, maxval=lw2, dtype=jnp.float32)
        ffn2_b = jnp.zeros((C_OUT,), jnp.float32)
        g1 = jnp.ones((C_IN,), jnp.float32)
        b1 = jnp.zeros((C_IN,), jnp.float32)
        g2 = jnp.ones((C_OUT,), jnp.float32)
        b2 = jnp.zeros((C_OUT,), jnp.float32)
        return {'x': x, 'W_Q': W_Q, 'W_K': W_K, 'W_V': W_V, 'W_O': W_O, 'ffn1_w': ffn1_w, 'ffn1_b': ffn1_b, 'ffn2_w': ffn2_w, 'ffn2_b': ffn2_b, 'g1': g1, 'b1': b1, 'g2': g2, 'b2': b2}
    _L0_conv_all = _L0_conv_setup()
    _L0_conv_in = {k: v for k, v in _L0_conv_all.items() if k in ('W_Q', 'W_K', 'W_V', 'W_O', 'ffn1_w', 'ffn1_b', 'ffn2_w', 'ffn2_b', 'g1', 'b1', 'g2', 'b2', )}
    del _L0_conv_all

    def _L1_conv_setup():
        import jax, jax.numpy as jnp
        from jax import lax
        import numpy as np
        DIM = 64
        K = 3
        K2 = K * K
        FGN_H = 32
        FFN_H = 128
        SE_R = 32
        B, H, W = (2, 256, 256)

        def layernorm(x, g, b):
            m = jnp.mean(x, axis=-1, keepdims=True)
            v = jnp.var(x, axis=-1, keepdims=True)
            return (x - m) / jnp.sqrt(v + 1e-05) * g + b

        def hardswish(x):
            return x * jnp.clip(x + 3.0, 0.0, 6.0) / 6.0

        def hardsigmoid(x):
            return jnp.clip(x + 3.0, 0.0, 6.0) / 6.0

        def conv1x1(x, w, b=None):
            y = jnp.einsum('oc,bchw->bohw', w, x)
            return y if b is None else y + b[None, :, None, None]

        def dwconv3(x, w):
            return lax.conv_general_dilated(x, w, window_strides=(1, 1), padding='SAME', dimension_numbers=('NCHW', 'OIHW', 'NCHW'), feature_group_count=x.shape[1])

        def dyn_filter(x, filt):
            b, c, h, w = x.shape
            p = K // 2
            xp = jnp.pad(x, ((0, 0), (0, 0), (p, p), (p, p)))
            patches = jnp.stack([xp[:, :, i:i + h, j:j + w] for i in range(K) for j in range(K)], axis=2)
            return jnp.sum(patches * filt, axis=2)
        key = jax.random.key(seed)
        ks = jax.random.split(key, 16)
        s = 0.05
        return {'x': jax.random.normal(ks[0], (B, DIM, H, W), jnp.float32), 'norm1_g': jnp.ones((DIM,), jnp.float32), 'norm1_b': jnp.zeros((DIM,), jnp.float32), 'fgn_l1_w': jax.random.normal(ks[1], (FGN_H, 2 * DIM), jnp.float32) * s, 'fgn_dw_w': jax.random.normal(ks[2], (FGN_H, 1, 3, 3), jnp.float32) * s, 'fgn_gc_w': jax.random.normal(ks[3], (FGN_H, FGN_H), jnp.float32) * s, 'fgn_gc_b': jnp.zeros((FGN_H,), jnp.float32), 'fgn_head_w': jax.random.normal(ks[4], (DIM * K2 * 2, FGN_H), jnp.float32) * s, 'fgn_head_b': jnp.zeros((DIM * K2 * 2,), jnp.float32), 'norm2_g': jnp.ones((DIM,), jnp.float32), 'norm2_b': jnp.zeros((DIM,), jnp.float32), 'ffn1_w': jax.random.normal(ks[5], (FFN_H, DIM), jnp.float32) * s, 'ffn_dw_w': jax.random.normal(ks[6], (FFN_H, 1, 3, 3), jnp.float32) * s, 'se1_w': jax.random.normal(ks[7], (SE_R, FFN_H), jnp.float32) * s, 'se1_b': jnp.zeros((SE_R,), jnp.float32), 'se2_w': jax.random.normal(ks[8], (FFN_H, SE_R), jnp.float32) * s, 'se2_b': jnp.zeros((FFN_H,), jnp.float32), 'ffn2_w': jax.random.normal(ks[9], (DIM, FFN_H), jnp.float32) * s, 'ffn2_b': jnp.zeros((DIM,), jnp.float32)}
    _L1_conv_all = _L1_conv_setup()
    _L1_conv_in = {k: v for k, v in _L1_conv_all.items() if k in ('norm1_g', 'norm1_b', 'fgn_l1_w', 'fgn_dw_w', 'fgn_gc_w', 'fgn_gc_b', 'fgn_head_w', 'fgn_head_b', 'norm2_g', 'norm2_b', 'ffn1_w', 'ffn_dw_w', 'se1_w', 'se1_b', 'se2_w', 'se2_b', 'ffn2_w', 'ffn2_b', )}
    del _L1_conv_all

    return {
        "x": x,
        "L0_conv_W_Q": _L0_conv_in["W_Q"],
        "L0_conv_W_K": _L0_conv_in["W_K"],
        "L0_conv_W_V": _L0_conv_in["W_V"],
        "L0_conv_W_O": _L0_conv_in["W_O"],
        "L0_conv_ffn1_w": _L0_conv_in["ffn1_w"],
        "L0_conv_ffn1_b": _L0_conv_in["ffn1_b"],
        "L0_conv_ffn2_w": _L0_conv_in["ffn2_w"],
        "L0_conv_ffn2_b": _L0_conv_in["ffn2_b"],
        "L0_conv_g1": _L0_conv_in["g1"],
        "L0_conv_b1": _L0_conv_in["b1"],
        "L0_conv_g2": _L0_conv_in["g2"],
        "L0_conv_b2": _L0_conv_in["b2"],
        "L1_conv_norm1_g": _L1_conv_in["norm1_g"],
        "L1_conv_norm1_b": _L1_conv_in["norm1_b"],
        "L1_conv_fgn_l1_w": _L1_conv_in["fgn_l1_w"],
        "L1_conv_fgn_dw_w": _L1_conv_in["fgn_dw_w"],
        "L1_conv_fgn_gc_w": _L1_conv_in["fgn_gc_w"],
        "L1_conv_fgn_gc_b": _L1_conv_in["fgn_gc_b"],
        "L1_conv_fgn_head_w": _L1_conv_in["fgn_head_w"],
        "L1_conv_fgn_head_b": _L1_conv_in["fgn_head_b"],
        "L1_conv_norm2_g": _L1_conv_in["norm2_g"],
        "L1_conv_norm2_b": _L1_conv_in["norm2_b"],
        "L1_conv_ffn1_w": _L1_conv_in["ffn1_w"],
        "L1_conv_ffn_dw_w": _L1_conv_in["ffn_dw_w"],
        "L1_conv_se1_w": _L1_conv_in["se1_w"],
        "L1_conv_se1_b": _L1_conv_in["se1_b"],
        "L1_conv_se2_w": _L1_conv_in["se2_w"],
        "L1_conv_se2_b": _L1_conv_in["se2_b"],
        "L1_conv_ffn2_w": _L1_conv_in["ffn2_w"],
        "L1_conv_ffn2_b": _L1_conv_in["ffn2_b"],
    }

def reference(x, L0_conv_W_Q, L0_conv_W_K, L0_conv_W_V, L0_conv_W_O, L0_conv_ffn1_w, L0_conv_ffn1_b, L0_conv_ffn2_w, L0_conv_ffn2_b, L0_conv_g1, L0_conv_b1, L0_conv_g2, L0_conv_b2, L1_conv_norm1_g, L1_conv_norm1_b, L1_conv_fgn_l1_w, L1_conv_fgn_dw_w, L1_conv_fgn_gc_w, L1_conv_fgn_gc_b, L1_conv_fgn_head_w, L1_conv_fgn_head_b, L1_conv_norm2_g, L1_conv_norm2_b, L1_conv_ffn1_w, L1_conv_ffn_dw_w, L1_conv_se1_w, L1_conv_se1_b, L1_conv_se2_w, L1_conv_se2_b, L1_conv_ffn2_w, L1_conv_ffn2_b):
    import jax
    import jax.numpy as jnp
    def _L0_conv_ref(x, W_Q, W_K, W_V, W_O, ffn1_w, ffn1_b, ffn2_w, ffn2_b, g1, b1, g2, b2):
        import jax, jax.numpy as jnp
        import numpy as np
        NUM_HEADS = 8
        HEAD_DIM = 8
        C_IN = 64
        C_OUT = 64
        EPS = 1e-05

        def _layernorm(x, g, b):
            m = jnp.mean(x, axis=-1, keepdims=True)
            v = jnp.mean((x - m) ** 2, axis=-1, keepdims=True)
            return (x - m) / jnp.sqrt(v + EPS) * g + b
        B, C, H, W = x.shape
        nh, hd = (NUM_HEADS, HEAD_DIM)
        x_nhwc = jnp.transpose(x, (0, 2, 3, 1))
        x_norm = _layernorm(x_nhwc, g1, b1)
        x_flat = x_norm.reshape(-1, C)
        Wq = W_Q.reshape(-1, hd * nh)
        Wk = W_K.reshape(-1, hd * nh)
        Wv = W_V.reshape(-1, hd * nh)
        Q = (x_flat @ Wq).reshape(B, H, W, nh, hd).transpose(0, 3, 1, 2, 4)
        K = (x_flat @ Wk).reshape(B, H, W, nh, hd).transpose(0, 3, 1, 2, 4)
        V = (x_flat @ Wv).reshape(B, H, W, nh, hd).transpose(0, 3, 1, 2, 4)
        scores = jnp.einsum('bnhwd,bmhwd->bnmhw', Q, K) / hd ** 0.5
        attn = jax.nn.softmax(scores, axis=2)
        a = jnp.einsum('bnmhw,bmhwd->bnhwd', attn, V)
        a = a.transpose(0, 2, 3, 1, 4).reshape(B, H, W, nh * hd)
        x_attn = a @ W_O
        y = jax.nn.relu(x_norm + x_attn)
        y = y.reshape(-1, 64)
        y = jax.nn.relu(y @ ffn1_w.T + ffn1_b)
        y = y @ ffn2_w.T + ffn2_b
        y = y.reshape(B, H, W, C_OUT)
        y = _layernorm(y, g2, b2)
        out = jax.nn.relu(jnp.transpose(y, (0, 3, 1, 2)) + x)
        return out

    def _L1_conv_ref(x, norm1_g, norm1_b, fgn_l1_w, fgn_dw_w, fgn_gc_w, fgn_gc_b, fgn_head_w, fgn_head_b, norm2_g, norm2_b, ffn1_w, ffn_dw_w, se1_w, se1_b, se2_w, se2_b, ffn2_w, ffn2_b):
        import jax, jax.numpy as jnp
        from jax import lax
        import numpy as np
        DIM = 64
        K = 3
        K2 = K * K
        FGN_H = 32
        FFN_H = 128
        SE_R = 32
        B, H, W = (2, 256, 256)

        def layernorm(x, g, b):
            m = jnp.mean(x, axis=-1, keepdims=True)
            v = jnp.var(x, axis=-1, keepdims=True)
            return (x - m) / jnp.sqrt(v + 1e-05) * g + b

        def hardswish(x):
            return x * jnp.clip(x + 3.0, 0.0, 6.0) / 6.0

        def hardsigmoid(x):
            return jnp.clip(x + 3.0, 0.0, 6.0) / 6.0

        def conv1x1(x, w, b=None):
            y = jnp.einsum('oc,bchw->bohw', w, x)
            return y if b is None else y + b[None, :, None, None]

        def dwconv3(x, w):
            return lax.conv_general_dilated(x, w, window_strides=(1, 1), padding='SAME', dimension_numbers=('NCHW', 'OIHW', 'NCHW'), feature_group_count=x.shape[1])

        def dyn_filter(x, filt):
            b, c, h, w = x.shape
            p = K // 2
            xp = jnp.pad(x, ((0, 0), (0, 0), (p, p), (p, p)))
            patches = jnp.stack([xp[:, :, i:i + h, j:j + w] for i in range(K) for j in range(K)], axis=2)
            return jnp.sum(patches * filt, axis=2)
        bsz, c, h, w = x.shape
        xn = layernorm(jnp.transpose(x, (0, 2, 3, 1)), norm1_g, norm1_b)
        xn = jnp.transpose(xn, (0, 3, 1, 2))
        fft_feat = jnp.fft.rfft2(xn.astype(jnp.float32), norm='ortho')
        mag = jnp.abs(fft_feat) + 1e-08
        phase = jnp.arctan2(fft_feat.imag, fft_feat.real)
        fgn_in = jnp.concatenate([mag, phase], axis=1)
        local = hardswish(dwconv3(conv1x1(fgn_in, fgn_l1_w), fgn_dw_w))
        gate = jax.nn.sigmoid(conv1x1(jnp.mean(local, axis=(2, 3), keepdims=True), fgn_gc_w, fgn_gc_b))
        filters = conv1x1(local * gate, fgn_head_w, fgn_head_b)
        hf, wf = mag.shape[-2:]
        mag_f, phase_f = jnp.split(filters, 2, axis=1)
        mag_f = jax.nn.softmax(mag_f.reshape(bsz, c, K2, hf, wf), axis=2)
        phase_f = jax.nn.softmax(phase_f.reshape(bsz, c, K2, hf, wf), axis=2)
        fm = dyn_filter(mag, mag_f)
        fp = dyn_filter(phase, phase_f)
        filtered = fm * jnp.cos(fp) + 1j * (fm * jnp.sin(fp))
        fft_out = jnp.fft.irfft2(filtered, s=(h, w), norm='ortho')
        x = x + fft_out
        xn2 = layernorm(jnp.transpose(x, (0, 2, 3, 1)), norm2_g, norm2_b)
        xn2 = jnp.transpose(xn2, (0, 3, 1, 2))
        y = hardswish(dwconv3(conv1x1(xn2, ffn1_w), ffn_dw_w))
        s = jnp.mean(y, axis=(2, 3), keepdims=True)
        s = jax.nn.relu(conv1x1(s, se1_w, se1_b))
        s = hardsigmoid(conv1x1(s, se2_w, se2_b))
        y = y * s
        y = conv1x1(y, ffn2_w, ffn2_b)
        return x + y

    def _gn(v, G=32, eps=1e-5):
        B_, C_, H_, W_ = v.shape
        g = v.reshape(B_, G, C_ // G, H_, W_)
        m = jnp.mean(g, axis=(2, 3, 4), keepdims=True)
        s = jnp.var(g, axis=(2, 3, 4), keepdims=True)
        return ((g - m) / jnp.sqrt(s + eps)).reshape(v.shape)

    def _ln_c(v, eps=1e-6):
        m = jnp.mean(v, axis=1, keepdims=True)
        s = jnp.var(v, axis=1, keepdims=True)
        return (v - m) / jnp.sqrt(s + eps)

    def _ln_t(v, eps=1e-5):
        m = jnp.mean(v, axis=-1, keepdims=True)
        s = jnp.var(v, axis=-1, keepdims=True)
        return (v - m) / jnp.sqrt(s + eps)

    def _to_tokens(v):
        B_, C_, H_, W_ = v.shape
        return v.reshape(B_, C_, H_ * W_).transpose(0, 2, 1)
    def _from_tokens(t, like):
        B_, C_, H_, W_ = like.shape
        return t.transpose(0, 2, 1).reshape(B_, C_, H_, W_)

    x = _L0_conv_ref(x, L0_conv_W_Q, L0_conv_W_K, L0_conv_W_V, L0_conv_W_O, L0_conv_ffn1_w, L0_conv_ffn1_b, L0_conv_ffn2_w, L0_conv_ffn2_b, L0_conv_g1, L0_conv_b1, L0_conv_g2, L0_conv_b2)
    x = _L1_conv_ref(x, L1_conv_norm1_g, L1_conv_norm1_b, L1_conv_fgn_l1_w, L1_conv_fgn_dw_w, L1_conv_fgn_gc_w, L1_conv_fgn_gc_b, L1_conv_fgn_head_w, L1_conv_fgn_head_b, L1_conv_norm2_g, L1_conv_norm2_b, L1_conv_ffn1_w, L1_conv_ffn_dw_w, L1_conv_se1_w, L1_conv_se1_b, L1_conv_se2_w, L1_conv_se2_b, L1_conv_ffn2_w, L1_conv_ffn2_b)
    return x


_drawn_inputs = setup_inputs


def setup_inputs(seed=0):
    import zlib

    import numpy as np

    out = dict(_drawn_inputs(seed))
    spreads = {'L0_conv_ffn1_b': (0.0, 0.1),
     'L0_conv_ffn2_b': (0.0, 0.1),
     'L0_conv_g1': (1.0, 0.2),
     'L0_conv_b1': (0.0, 0.1),
     'L0_conv_g2': (1.0, 0.2),
     'L0_conv_b2': (0.0, 0.1),
     'L1_conv_norm1_g': (1.0, 0.2),
     'L1_conv_norm1_b': (0.0, 0.49),
     'L1_conv_fgn_gc_b': (0.0, 0.8),
     'L1_conv_fgn_head_b': (0.0, 0.1),
     'L1_conv_norm2_g': (1.0, 0.6),
     'L1_conv_norm2_b': (0.0, 0.8),
     'L1_conv_se1_b': (0.0, 0.8),
     'L1_conv_se2_b': (0.0, 0.8),
     'L1_conv_ffn2_b': (0.0, 0.8)}
    factors = {'L1_conv_fgn_l1_w': 3.267,
     'L1_conv_fgn_dw_w': 2.894,
     'L1_conv_fgn_gc_w': 8.0,
     'L1_conv_fgn_head_w': 2.736,
     'L1_conv_ffn1_w': 8.0,
     'L1_conv_ffn_dw_w': 8.0,
     'L1_conv_se1_w': 8.0,
     'L1_conv_se2_w': 8.0,
     'L1_conv_ffn2_w': 8.0}
    for name, (base, spread) in spreads.items():
        noise = np.random.default_rng([zlib.crc32(name.encode()), seed]).standard_normal(out[name].shape)
        drawn = base * np.exp(spread * noise) if base else spread * noise
        out[name] = jnp.asarray(drawn.astype(out[name].dtype))
    for name, factor in factors.items():
        out[name] = (out[name] * factor).astype(out[name].dtype)
    return out
```

```python
from contextlib import ExitStack

import concourse.bass as bass
from concourse import mybir

F32 = mybir.dt.float32
ALU = mybir.AluOpType
ACT = mybir.ActivationFunctionType
X = mybir.AxisListType.X

P = 128
C = 64
H = W = 128
KX = W // 2 + 1
KG = 33
NH, HD = 8, 8
RPC = 4
CH = RPC * W
NCH = (H // 2) // RPC
NY = 32
FG = 32
NQ = 4
QY = H // NQ
KR = 5
NK = KX // KR
FN = KR * QY
T9 = 9
PI = 3.1415925025939941
HALF_PI = 1.5707963267948966
TINY = 1e-30
SET_LN_EXP = 6

VECS = ["g1", "b1", "f1b", "f2b", "g2", "b2", "n1g", "n1b", "n2g", "n2b", "ob", "gcb", "se2b",
        "se1b", "eps", "half_pi", "three", "tiny_mag", "pi", "se2b3", "f2c"]
NLOADED = VECS.index("eps")


def build(nc, x, vec, tabs, wqkv, wo, f1t, f2, l1t, dwt, gct, head, head_b, w1t, d9, se1t, se2t, w2t, ones, out):
    n_img = x.shape[0]
    ctx = ExitStack()
    with ctx:
        def sb(name, n, parts=P):
            return ctx.enter_context(nc.sbuf_tensor(name, [parts, n], F32))

        def sem(name):
            return ctx.enter_context(nc.semaphore(name))

        TB = sb("tables", 3 * P + 130 + 3 * 256 + P)
        o = [0]

        def tab(n):
            o[0] += n
            return TB[:, o[0] - n:o[0]]
        IDN, CEN, ONE = tab(P), tab(P), tab(P)
        DFTW = tab(130)
        DRE, DIM = tab(256), tab(256)
        ICS = tab(256)
        IFW = tab(P)
        V = sb("vectors", len(VECS))
        WQ = sb("w_qkv", 3 * 2 * C)
        WO = sb("w_o", P)
        W1 = sb("w_ffn1", P)
        W2 = sb("w_ffn2", P)
        LW = sb("w_local", NQ * P)
        DW = sb("w_dw", T9)
        GC = sb("w_gate", P)
        HW = sb("w_head", T9 * P)
        CWP = sb("w_conv_pair", 3 * P)
        CWS = sb("w_conv_single", 3 * P, C)
        SE1 = sb("w_se1", FG)
        SE2 = sb("w_se2", P, FG)
        WF = sb("w_out", 2 * P)
        WS = sb("w_out_gated", 2 * P)
        SM = sb("small", 64)
        XC = sb("x_chan", NCH * CH)
        AR = sb("arena", 39000)
        PS = ctx.enter_context(nc.psum_tensor("ps", [P, 8, 512], F32))

        def vec_of(name, parts=P):
            i = VECS.index(name)
            return V[0:parts, i:i + 1]

        def area(off, n):
            return AR[:, off:off + n]

        XP1 = area(0, 8192)
        o[0] = 8192

        def part(n):
            o[0] += n
            return area(o[0] - n, n)
        PROD = part(RPC * 2 * 512)
        PV = [part(RPC * 2 * 512) for _ in range(2)]
        QS = [part(RPC * 384) for _ in range(2)]
        XN = [part(CH) for _ in range(4)]
        SC, EX, PB, OS, Y0, Y1 = (part(CH) for _ in range(6))
        SQ = [part(CH) for _ in range(3)]
        RS = [part(CH) for _ in range(3)]
        XH = [part(CH) for _ in range(3)]
        XT = part(CH)
        MX, SU, RI = part(C), part(C), part(C)
        AF = area(8192, 2 * KG * P)
        RE, IM, MG, TT = (area(16640 + i * KG * H, KG * H) for i in range(4))
        MPW = H + 2
        MP = area(0, (KX + 2) * MPW)
        LPW = QY + 2
        LP = area(8710, (KX + 2) * LPW)
        AC, UU = area(10988, KX * QY), area(13068, KX * QY)
        LOC = area(16640, NQ * KX * QY)
        FMP = area(24960, KX * H)
        EE = [area(33280 + i * T9 * FN, T9 * FN) for i in range(2)]
        PD = [area(o_, T9 * FN) for o_ in (36160, 10988, 12428, 13868)]
        MXF, DEN = ([area(37600 + (2 * j + i) * FN, FN) for i in range(2)] for j in range(2))
        RDN = [area(37600 + (4 + i) * FN, FN) for i in range(4)]
        FM2, FP2 = area(0, KG * H), area(4224, KG * H)
        SN, CO = area(8448, KG * H), area(12672, KG * H)
        ZA, ZB = area(16896, C * P), area(25088, C * P)
        BF = area(0, C * P)
        XPW = W + 2
        XP = area(0, (H + 2) * XPW)
        HID = area(16900, H * W)
        o[0] = 33284
        SQE, RSE, XHE = part(CH), part(CH), part(CH)
        XNE = [part(CH) for _ in range(2)]
        UE = [part(CH) for _ in range(2)]
        OB = [part(CH) for _ in range(2)]
        SUMH = SM[:, 8:8 + NY]
        D9 = area(0, T9 * P)
        W1D = area(T9 * P, P)
        WN = area((T9 + 1) * P, P)

        s_x_loaded = sem("s_x_loaded")
        s_scaled1 = sem("s_scaled1")
        s_centred1 = sem("s_centred1")
        s_attn_relu = sem("s_attn_relu")
        s_ffn1_made = sem("s_ffn1_made")
        s_normed3 = sem("s_normed3")
        s_ffn1_relu = sem("s_ffn1_relu")
        s_transposed = sem("s_transposed")
        s_square1 = sem("s_square1")
        s_var1 = sem("s_var1")
        s_scaled2 = sem("s_scaled2")
        s_ffn2_centred = sem("s_ffn2_centred")
        s_square2 = sem("s_square2")
        s_scaled3 = sem("s_scaled3")
        s_var2 = sem("s_var2")
        s_normed1 = sem("s_normed1")
        s_qkv_copied = sem("s_qkv_copied")
        s_qkv_made = sem("s_qkv_made")
        s_pv_halved = sem("s_pv_halved")
        s_attn_copied = sem("s_attn_copied")
        s_layer0_out = sem("s_layer0_out")
        s_centred3 = sem("s_centred3")
        s_attn_summed = sem("s_attn_summed")
        s_square3 = sem("s_square3")
        s_var3 = sem("s_var3")
        s_pixels_copied = sem("s_pixels_copied")
        s_attn_projected = sem("s_attn_projected")
        s_ln1 = sem("s_ln1")
        s_rstd1 = sem("s_rstd1")
        s_ln2 = sem("s_ln2")
        s_rstd2 = sem("s_rstd2")
        s_scores_shifted = sem("s_scores_shifted")
        s_score_exp = sem("s_score_exp")
        s_pv_products = sem("s_pv_products")
        s_residual_added = sem("s_residual_added")
        s_ln3 = sem("s_ln3")
        s_rstd3 = sem("s_rstd3")
        s_qk_products = sem("s_qk_products")
        s_scores = sem("s_scores")
        s_score_max = sem("s_score_max")
        s_exp_sum = sem("s_exp_sum")
        s_exp_sum_inv = sem("s_exp_sum_inv")
        s_probs = sem("s_probs")
        s_dft_w_made = sem("s_dft_w_made")
        s_dft_h_copied = sem("s_dft_h_copied")
        s_dft_h_made = sem("s_dft_h_made")
        s_mag_squared = sem("s_mag_squared")
        s_mag_and_abs = sem("s_mag_and_abs")
        s_re_im_squares = sem("s_re_im_squares")
        s_phase_den = sem("s_phase_den")
        s_mag_done = sem("s_mag_done")
        s_half_tan = sem("s_half_tan")
        s_half_angle = sem("s_half_angle")
        s_angle_twice = sem("s_angle_twice")
        s_phase_den_inv = sem("s_phase_den_inv")
        s_im_sign = sem("s_im_sign")
        s_borders_zeroed = sem("s_borders_zeroed")
        s_phase_done = sem("s_phase_done")
        s_spectrum_padded = sem("s_spectrum_padded")
        s_local_copied = sem("s_local_copied")
        s_local_made = sem("s_local_made")
        s_local_sum = sem("s_local_sum")
        s_gate_logit = sem("s_gate_logit")
        s_dw_taps = sem("s_dw_taps")
        s_local_relu3 = sem("s_local_relu3")
        s_gate = sem("s_gate")
        s_local_swish = sem("s_local_swish")
        s_local_gated = sem("s_local_gated")
        s_local_moved = sem("s_local_moved")
        s_filt_shifted = sem("s_filt_shifted")
        s_filt_logits = sem("s_filt_logits")
        s_filt_products_paired = sem("s_filt_products_paired")
        s_filtered = sem("s_filtered")
        s_filt_weighted = sem("s_filt_weighted")
        s_filt_max = sem("s_filt_max")
        s_filt_exp = sem("s_filt_exp")
        s_filt_sum_inv = sem("s_filt_sum_inv")
        s_filt_sum = sem("s_filt_sum")
        s_filt_products = sem("s_filt_products")
        s_filt_ln = sem("s_filt_ln")
        s_filtered_moved = sem("s_filtered_moved")
        s_im_made = sem("s_im_made")
        s_re_made = sem("s_re_made")
        s_spec_transposed = sem("s_spec_transposed")
        s_idft_h_made = sem("s_idft_h_made")
        s_x2_done = sem("s_x2_done")
        s_idft_w_made = sem("s_idft_w_made")
        s_angle_clamped = sem("s_angle_clamped")
        s_sin_made = sem("s_sin_made")
        s_angle_abs = sem("s_angle_abs")
        s_cos_made = sem("s_cos_made")
        s_image_borders_zeroed = sem("s_image_borders_zeroed")
        s_hidden_done = sem("s_hidden_done")
        s_conv_made = sem("s_conv_made")
        s_scaled4 = sem("s_scaled4")
        s_centred4 = sem("s_centred4")
        s_square4 = sem("s_square4")
        s_var4 = sem("s_var4")
        s_hidden_sum = sem("s_hidden_sum")
        s_se1_made = sem("s_se1_made")
        s_se1_relu = sem("s_se1_relu")
        s_se2_made = sem("s_se2_made")
        s_w_out_scaled = sem("s_w_out_scaled")
        s_projected = sem("s_projected")
        s_out_ready = sem("s_out_ready")
        s_conv_relu3 = sem("s_conv_relu3")
        s_ln4 = sem("s_ln4")
        s_rstd4 = sem("s_rstd4")
        s_normed4 = sem("s_normed4")
        s_se2_relu = sem("s_se2_relu")
        s_se_gate = sem("s_se_gate")
        s_weights_zeroed = sem("s_weights_zeroed")
        s_weights_loaded = sem("s_weights_loaded")
        s_weights_made = sem("s_weights_made")
        s_vec_constants = sem("s_vec_constants")
        s_ffn2_folded = sem("s_ffn2_folded")
        s_dft_w_copied = [sem(f"s_dft_w_copied{i}") for i in range(2)]
        s_idft_h_copied = [sem(f"s_idft_h_copied{i}") for i in range(2)]
        s_spec_copied = [sem(f"s_spec_copied{i}") for i in range(2)]
        s_rows_moved = [sem(f"s_rows_moved{i}") for i in range(4)]
        s_written = [sem(f"s_written{i}") for i in range(2)]

        def bank(b, n=512, off=0):
            return PS[:, b, off:off + n]

        lay3 = lambda a, n: a.rearrange("p (a b) -> p a b", b=n)

        def later(n, least=1):
            return not isinstance(n, int) or n >= least

        def a_pe(pe, im, k, u, live):
            qk, _, at, ff, tr = live
            if qk:
                if isinstance(k, int) and k == 0:
                    pe.wait_ge(s_x_loaded, (im + 1) * (NCH * 16))
                if later(k):
                    pe.wait_ge(s_scaled1, im * NCH + k)
                pe.matmul(bank(0), CEN, XC[:, bass.ds(k * CH, CH)], start=True, stop=True).then_inc(s_centred1, 1)
            if ff:
                pe.wait_ge(s_attn_relu, im * NCH + k - 2)
                pe.matmul(bank(5), W1[:, :], Y0, start=True, stop=True).then_inc(s_ffn1_made, 1)
            if tr:
                pe.wait_ge(s_normed3, im * NCH + k - 3)
                if ff:
                    pe.wait_ge(s_ffn1_relu, im * NCH + k - 2)
                for r in range(RPC):
                    i = pe.transpose(bank(5, W, r * W), XT[:, r * W:(r + 1) * W], IDN)
                i.then_inc(s_transposed, 1)
            if qk:
                pe.wait_ge(s_square1, im * NCH + k + 1)
                pe.matmul(bank(1), ONE, SQ[0], start=True, stop=True).then_inc(s_var1, 1)
            if ff:
                kk = k - 3
                pe.wait_ge(s_ffn1_relu, im * NCH + kk + 1)
                if later(kk):
                    pe.wait_ge(s_scaled2, im * NCH + kk)
                pe.matmul(bank(6), W2[:, :], Y1, start=True, stop=True).then_inc(s_ffn2_centred, 1)
                pe.wait_ge(s_square2, im * NCH + kk + 1)
                if later(kk):
                    pe.wait_ge(s_scaled3, im * NCH + kk)
                pe.matmul(bank(7), ONE, SQ[1], start=True, stop=True).then_inc(s_var2, 1)
            if qk:
                pe.wait_ge(s_normed1, im * NCH + k + 1)
                for r in range(RPC):
                    n = (RPC * k) + r - 1
                    if not isinstance(k, int) or n >= 1:
                        pe.wait_ge(s_qkv_copied, im * (NCH * RPC) + n)
                    pe.matmul(bank(2 + r % 2, 384), XN[u % 4][:, r * W:(r + 1) * W], WQ[:, :],
                              start=True, stop=True).then_inc(s_qkv_made, 1)

            def sum_values(rows):
                pvv = PV[u % 2].rearrange("p (m r c) -> p r m c", r=RPC, m=NH)
                for r in rows:
                    for m in range(NH // 2):
                        i = pe.matmul(bank(4, W, r * W), pvv[:, r, m], IDN, start=(r == 0 and m == 0),
                                      stop=(r == RPC - 1 and m == NH // 2 - 1), skip_group_check=True)
                return i
            if at:
                pe.wait_ge(s_pv_halved, im * NCH + k - 1)
                if later(k - 2):
                    pe.wait_ge(s_attn_copied, im * NCH + k - 2)
                sum_values((0, 1))
            if ff:
                kk = k - 3
                pe.wait_ge(s_layer0_out, im * NCH + kk + 1)
                pe.matmul(bank(7), CEN, XC[:, bass.ds(kk * CH, CH)], start=True, stop=True).then_inc(s_centred3, 1)
            if at:
                sum_values((2, 3)).then_inc(s_attn_summed, 1)
            if ff:
                pe.wait_ge(s_square3, im * NCH + k - 2)
                pe.matmul(bank(1), ONE, SQ[2], start=True, stop=True).then_inc(s_var3, 1)
            if at:
                pe.wait_ge(s_attn_copied, im * NCH + k - 1)
                if tr:
                    pe.wait_ge(s_pixels_copied, im * NCH + k - 3)
                pe.matmul(bank(5), WO[:, :], OS, start=True, stop=False)
                pe.matmul(bank(5), IDN, XN[(u - 2) % 4], start=False, stop=True).then_inc(s_attn_projected, 1)

        def rstd(act, im, k, src, dst, var, last_read, ln, done):
            act.wait_ge(var, im * NCH + k + 1)
            if later(k):
                act.wait_ge(last_read, im * NCH + k)
            act.activation(dst, src, ACT.Ln, bias=vec_of("eps")).then_inc(ln, 1)
            act.wait_ge(ln, im * NCH + k + 1)
            act.activation(dst, dst, ACT.Exp, scale=-0.5).then_inc(done, 1)

        def a_act(act, im, k, u, live):
            qk, sm, at, ff, tr = live
            if qk:
                act.wait_ge(s_centred1, im * NCH + k + 1)
                act.activation(SQ[0], bank(0), ACT.Square).then_inc(s_square1, 1)
            if ff:
                act.wait_ge(s_ffn1_made, im * NCH + k - 2)
                act.activation(Y1, bank(5), ACT.Relu, bias=vec_of("f1b")).then_inc(s_ffn1_relu, 1)
            if tr:
                kk = k - 4
                act.wait_ge(s_transposed, im * NCH + kk + 1)
                dst = XP1.rearrange("p (s h c) -> p s h c", s=2, c=C)[:, :, bass.ds(kk * RPC, RPC), :]
                act.activation(dst, bank(5).rearrange("p (r s c) -> p s r c", r=RPC, s=2), ACT.Copy).then_inc(s_pixels_copied, 1)
            if qk:
                rstd(act, im, k, bank(1), RS[0], s_var1, s_scaled1, s_ln1, s_rstd1)
            if ff:
                act.wait_ge(s_ffn2_centred, im * NCH + k - 2)
                act.activation(SQ[1], bank(6), ACT.Square, bias=vec_of("f2c")).then_inc(s_square2, 1)
            if qk:
                act.wait_ge(s_scaled1, im * NCH + k + 1)
                act.activation(XN[u % 4], XH[0], ACT.Identity, bias=vec_of("b1")).then_inc(s_normed1, 1)
            if ff:
                rstd(act, im, k - 3, bank(7), RS[1], s_var2, s_scaled2, s_ln2, s_rstd2)
            if sm:
                kk = k - 1
                act.wait_ge(s_scores_shifted, im * NCH + kk + 1)
                act.activation(EX, SC, ACT.Exp, scale=HD ** -0.5).then_inc(s_score_exp, 1)

            def take_qkv(rows):
                qsv = QS[u % 2].rearrange("p (j r c) -> p r j c", j=3, r=RPC)
                for r in rows:
                    act.wait_ge(s_qkv_made, im * (NCH * RPC) + RPC * k + r + 1)
                    act.activation(qsv[:, r], bank(2 + r % 2, 384).rearrange("p (j c) -> p j c", j=3),
                                   ACT.Copy).then_inc(s_qkv_copied, 1)
            if qk:
                if later(k, 2):
                    act.wait_ge(s_pv_products, im * NCH + k - 1)
                take_qkv((0, 1))
            if ff:
                kk = k - 3
                act.wait_ge(s_residual_added, im * NCH + kk + 1)
                act.activation(XC[:, bass.ds(kk * CH, CH)], XH[1], ACT.Relu, bias=vec_of("b2")).then_inc(s_layer0_out, 1)
            if qk:
                take_qkv((2, 3))
            if ff:
                act.wait_ge(s_centred3, im * NCH + k - 2)
                act.activation(SQ[2], bank(7), ACT.Square).then_inc(s_square3, 1)
            if at:
                act.wait_ge(s_attn_summed, im * NCH + k - 1)
                act.activation(OS, bank(4), ACT.Copy).then_inc(s_attn_copied, 1)
            if ff:
                rstd(act, im, k - 3, bank(1), RS[2], s_var3, s_scaled3, s_ln3, s_rstd3)
            if at:
                act.wait_ge(s_attn_projected, im * NCH + k - 1)
                act.activation(Y0, bank(5), ACT.Relu).then_inc(s_attn_relu, 1)
            if ff:
                act.wait_ge(s_scaled3, im * NCH + k - 2)
                act.activation(XT, XH[2], ACT.Identity, bias=vec_of("n1b")).then_inc(s_normed3, 1)

        def a_dve(dve, im, k, u, live):
            qk, sm, _, ff, _ = live
            if sm:
                kk = k - 1
                dve.wait_ge(s_qk_products, im * NCH + kk + 1)
                if later(kk):
                    dve.wait_ge(s_score_exp, im * NCH + kk)
                dve.tensor_reduce(SC, lay3(PROD, HD), X, ALU.add).then_inc(s_scores, 1)
            if qk:
                dve.wait_ge(s_rstd1, im * NCH + k + 1)
                if later(k):
                    dve.wait_ge(s_normed1, im * NCH + k)
                dve.scalar_tensor_tensor(out=XH[0], in0=bank(0), scalar=vec_of("g1"), in1=RS[0],
                                         op0=ALU.mult, op1=ALU.mult).then_inc(s_scaled1, 1)
            if sm:
                kk = k - 1
                sc = lay3(SC, NH)
                dve.wait_ge(s_scores, im * NCH + kk + 1)
                dve.tensor_reduce(MX, sc, X, ALU.max).then_inc(s_score_max, 1)
                dve.wait_ge(s_score_max, im * NCH + kk + 1)
                dve.tensor_tensor(sc, sc, MX.unsqueeze(2).broadcast_to([P, C, NH]), ALU.subtract).then_inc(s_scores_shifted, 1)
            if ff:
                kk = k - 3
                dve.wait_ge(s_rstd2, im * NCH + kk + 1)
                if later(kk):
                    dve.wait_ge(s_layer0_out, im * NCH + kk)
                dve.scalar_tensor_tensor(out=XH[1], in0=bank(6), scalar=vec_of("f2c"), in1=RS[1],
                                         op0=ALU.add, op1=ALU.mult).then_inc(s_scaled2, 1)
                dve.wait_ge(s_scaled2, im * NCH + kk + 1)
                dve.scalar_tensor_tensor(out=XH[1], in0=XH[1], scalar=vec_of("g2"), in1=XC[:, bass.ds(kk * CH, CH)],
                                         op0=ALU.mult, op1=ALU.add).then_inc(s_residual_added, 1)
            if sm:
                kk = k - 1
                ex = lay3(EX, NH)
                dve.wait_ge(s_score_exp, im * NCH + kk + 1)
                dve.tensor_reduce(SU, ex, X, ALU.add).then_inc(s_exp_sum, 1)
                dve.wait_ge(s_exp_sum, im * NCH + kk + 1)
                dve.reciprocal(RI, SU).then_inc(s_exp_sum_inv, 1)
                dve.wait_ge(s_exp_sum_inv, im * NCH + kk + 1)
                if later(kk):
                    dve.wait_ge(s_pv_products, im * NCH + kk)
                dve.tensor_tensor(lay3(PB, NH), ex, RI.unsqueeze(2).broadcast_to([P, C, NH]), ALU.mult).then_inc(s_probs, 1)
            if qk:
                q = QS[u % 2].rearrange("p (j g n d) -> p j g n d", j=3, g=2 * RPC, n=NH)
                dve.wait_ge(s_qkv_copied, im * (NCH * RPC) + RPC * (k + 1))
                if later(k):
                    dve.wait_ge(s_scores, im * NCH + k)
                pr = PROD.rearrange("p (g n m d) -> p g n m d", g=2 * RPC, n=NH, m=NH)
                shape = [P, 2 * RPC, NH, NH, HD]
                dve.tensor_tensor(pr, q[:, 0].unsqueeze(3).broadcast_to(shape),
                                  q[:, 1].unsqueeze(2).broadcast_to(shape), ALU.mult).then_inc(s_qk_products, 1)
            if ff:
                kk = k - 3
                dve.wait_ge(s_rstd3, im * NCH + kk + 1)
                if later(kk):
                    dve.wait_ge(s_normed3, im * NCH + kk)
                dve.scalar_tensor_tensor(out=XH[2], in0=bank(7), scalar=vec_of("n1g"), in1=RS[2],
                                         op0=ALU.mult, op1=ALU.mult).then_inc(s_scaled3, 1)

        def a_pool(pool, im, k, u, live):
            if live[1]:
                kk = k - 1
                pool.wait_ge(s_probs, im * NCH + kk + 1)
                if later(kk, 2):
                    pool.wait_ge(s_attn_summed, im * NCH + kk - 1)
                v = QS[(u - 1) % 2].rearrange("p (j r s m d) -> p j r s m d", j=3, r=RPC, s=2, m=NH)[:, 2]
                pb = PB.rearrange("p (r s n m) -> p r s n m", r=RPC, s=2, n=NH)
                tile_ = PV[(u - 1) % 2]
                pv = tile_.rearrange("p (m r s n d) -> p r s n m d", r=RPC, m=NH, s=2, n=NH)
                shape = [P, 2, NH, NH, HD]
                for r in range(RPC):
                    i = pool.tensor_tensor(pv[:, r], pb[:, r].unsqueeze(4).broadcast_to(shape),
                                           v[:, r].unsqueeze(2).broadcast_to(shape), ALU.mult)
                i.then_inc(s_pv_products, 1)
                pool.wait_ge(s_pv_products, im * NCH + kk + 1)
                n = NH // 2 * CH
                pool.tensor_tensor(tile_[:, 0:n], tile_[:, 0:n], tile_[:, n:2 * n], ALU.add).then_inc(s_pv_halved, 1)

        def pipeline(eng, stage, im):
            live = lambda k: tuple(0 <= k - j < NCH for j in range(5))
            for k in range(4):
                stage(eng, im, k, k % 4, live(k))
            with eng.Fori(1, NCH // 4) as k4:
                for u in range(4):
                    stage(eng, im, k4 * 4 + u, u, (True,) * 5)
            for k in range(NCH, NCH + 4):
                stage(eng, im, k, k % 4, live(k))

        B1 = [(i, min(3, C - i)) for i in range(0, C, 3)]
        B2 = [(i, min(4, KG - i)) for i in range(0, KG, 4)]
        NB1, NB2 = len(B1), len(B2)
        GP = 3
        NP = NB2 // GP
        PIECES = [(B2[GP * p][0], sum(n for _, n in B2[GP * p:GP * p + GP])) for p in range(NP)]
        af = AF.rearrange("p (r k m) -> p r k m", r=2, k=KG)
        afc = AF.rearrange("p (r k g c) -> p r k g c", r=2, k=KG, g=2)

        def piece(a, p):
            return a[:, PIECES[p][0] * H:(PIECES[p][0] + PIECES[p][1]) * H]

        def b_pe(pe, im):
            pe.wait_ge(s_pixels_copied, (im + 1) * NCH)
            xp = XP1.rearrange("p (h c) -> p h c", c=C)
            for g, (c0, n) in enumerate(B1):
                if g >= 4:
                    pe.wait_ge(s_dft_w_copied[g % 2], im * (NB1 // 2) + (g - 4) // 2 + 1)
                for j in range(n):
                    i = pe.matmul(bank(g % 4, 130, j * 130), xp[:, :, c0 + j], DFTW, start=(j == 0),
                                  stop=(j == n - 1), skip_group_check=True)
                i.then_inc(s_dft_w_made, 1)
            pe.wait_ge(s_dft_w_copied[0], (im + 1) * (NB1 // 2))
            pe.wait_ge(s_dft_w_copied[1], (im + 1) * (NB1 // 2))
            for g, (k0, n) in enumerate(B2):
                if g >= 4:
                    pe.wait_ge(s_dft_h_copied, im * NB2 + g - 3)
                for j in range(n):
                    a, b = af[:, 0, k0 + j], af[:, 1, k0 + j]
                    for ri in range(2):
                        dst = bank(2 * (g % 4) + ri, H, j * H)
                        pe.matmul(dst, a, DRE[:, ri * H:(ri + 1) * H], start=(j == 0), stop=False,
                                  skip_group_check=True)
                        i = pe.matmul(dst, b, DIM[:, ri * H:(ri + 1) * H], start=False, stop=(j == n - 1),
                                      skip_group_check=True)
                i.then_inc(s_dft_h_made, 1)

        def b1_evac(eng, im, me, copy):
            for g, (c0, n) in enumerate(B1):
                if g % 2 == me:
                    eng.wait_ge(s_dft_w_made, im * NB1 + g + 1)
                    src = bank(g % 4, n * 130).rearrange("p (c r k) -> p r k c", c=n, r=2)
                    for h in range(2):
                        i = copy(afc[:, :, :, h, c0:c0 + n], src[:, :, 32 * h:32 * h + KG])
                    i.then_inc(s_dft_w_copied[me], 1)

        def b_act(act, im):
            b1_evac(act, im, 0, lambda o_, i_: act.activation(o_, i_, ACT.Copy))

            def root(p):
                act.wait_ge(s_mag_squared, im * NP + p + 1)
                act.activation(piece(MG, p), piece(MG, p), ACT.Sqrt)
                act.activation(piece(TT, p), piece(IM, p), ACT.Abs).then_inc(s_mag_and_abs, 1)
            for g, (k0, n) in enumerate(B2):
                act.wait_ge(s_dft_h_made, im * NB2 + g + 1)
                act.activation(RE[:, k0 * H:(k0 + n) * H], bank(2 * (g % 4), n * H), ACT.Copy)
                act.activation(IM[:, k0 * H:(k0 + n) * H], bank(2 * (g % 4) + 1, n * H), ACT.Copy).then_inc(s_dft_h_copied, 1)
                if g % GP == GP - 1:
                    p = g // GP
                    act.wait_ge(s_dft_h_copied, im * NB2 + g + 1)
                    act.activation(piece(MG, p), piece(RE, p), ACT.Square)
                    act.activation(piece(TT, p), piece(IM, p), ACT.Square).then_inc(s_re_im_squares, 1)
                    if p >= 1:
                        root(p - 1)
            root(NP - 1)
            for p in range(NP):
                act.wait_ge(s_phase_den, im * NP + p + 1)
                act.activation(piece(MG, p), piece(MG, p), ACT.Identity, bias=vec_of("tiny_mag")).then_inc(s_mag_done, 1)
                act.wait_ge(s_half_tan, im * NP + p + 1)
                act.activation(piece(RE, p), piece(RE, p), ACT.Arctan).then_inc(s_half_angle, 1)
                act.wait_ge(s_half_angle, im * NP + p + 1)
                act.activation(piece(RE, p), piece(RE, p), ACT.Identity, bias=vec_of("pi"), scale=-4.0).then_inc(s_angle_twice, 1)

        def b_dve(dve, im):
            b1_evac(dve, im, 1, lambda o_, i_: dve.tensor_copy(o_, i_))
            for p in range(NP):
                dve.wait_ge(s_mag_and_abs, im * NP + p + 1)
                dve.scalar_tensor_tensor(out=piece(TT, p), in0=piece(TT, p), scalar=TINY, in1=piece(MG, p),
                                         op0=ALU.add, op1=ALU.add).then_inc(s_phase_den, 1)
                dve.wait_ge(s_phase_den, im * NP + p + 1)
                dve.reciprocal(piece(TT, p), piece(TT, p)).then_inc(s_phase_den_inv, 1)
                dve.tensor_scalar(piece(IM, p), piece(IM, p), 0.0, 0.5, ALU.is_ge, ALU.subtract).then_inc(s_im_sign, 1)
                dve.wait_ge(s_phase_den_inv, im * NP + p + 1)
                dve.scalar_tensor_tensor(out=piece(RE, p), in0=piece(RE, p), scalar=TINY, in1=piece(TT, p),
                                         op0=ALU.add, op1=ALU.mult).then_inc(s_half_tan, 1)
                if p == 0:
                    dve.wait_ge(s_dft_h_made, (im + 1) * NB2)
                    dve.memset(mp[:, 0:KX + 2:KX + 1, :], 0.0).then_inc(s_borders_zeroed, 1)
                    dve.memset(mp[:, 1:KX + 1, 0:MPW:MPW - 1], 0.0).then_inc(s_borders_zeroed, 1)
                    dve.memset(lp[:, 0:KX + 2:KX + 1, :], 0.0).then_inc(s_borders_zeroed, 1)

        def b_pool(pool, im):
            for p in range(NP):
                pool.wait_ge(s_re_im_squares, im * NP + p + 1)
                pool.tensor_tensor(piece(MG, p), piece(MG, p), piece(TT, p), ALU.add).then_inc(s_mag_squared, 1)
            for p in range(NP):
                pool.wait_ge(s_angle_twice, im * NP + p + 1)
                pool.wait_ge(s_im_sign, im * NP + p + 1)
                pool.tensor_tensor(piece(RE, p), piece(RE, p), piece(IM, p), ALU.mult).then_inc(s_phase_done, 1)

        mp = MP.rearrange("p (k y) -> p k y", y=MPW)
        lp = LP.rearrange("p (k y) -> p k y", y=LPW)
        xpv = XP.rearrange("p (r c) -> p r c", c=XPW)

        def b_sync(sp, im):
            sp.wait_ge(s_dft_h_made, (im + 1) * NB2)
            for p, (k0, n) in enumerate(PIECES):
                for lo, src, ready in ((0, MG, s_mag_done), (C, RE, s_phase_done)):
                    sp.wait_ge(ready, im * NP + p + 1)
                    v = lay3(src, H)
                    k1 = max(k0, 1)
                    sp.dma_start(mp[lo:lo + C, 1 + k0:1 + k0 + n, 1:1 + H], v[0:C, k0:k0 + n]).then_inc(s_spectrum_padded, 16)
                    sp.dma_start(mp[lo:lo + C, 33 + k1:33 + k0 + n, 1:1 + H], v[C:P, k1:k0 + n]).then_inc(s_spectrum_padded, 16)

        C1R = 13
        NC1 = KX // C1R

        def c_pe(pe, im):
            pe.wait_ge(s_spectrum_padded, (im + 1) * (64 * NP))
            pe.wait_ge(s_borders_zeroed, (im + 1) * 3)
            for g in range(NC1):
                if g >= 2:
                    pe.wait_ge(s_local_copied, im * NC1 + g - 1)
                for q in range(NQ):
                    i = pe.matmul(bank(g % 2, C1R * LPW), LW[:, q * P:(q + 1) * P],
                                  mp[:, 1 + g * C1R:1 + (g + 1) * C1R, q * QY:q * QY + LPW],
                                  start=(q == 0), stop=(q == NQ - 1))
                i.then_inc(s_local_made, 1)
            pe.wait_ge(s_local_sum, im + 1)
            pe.matmul(bank(2, 1), GC[:, :], SM[:, 0:1], start=True, stop=True).then_inc(s_gate_logit, 1)

        def c_act(act, im):
            for g in range(NC1):
                act.wait_ge(s_local_made, im * NC1 + g + 1)
                act.activation(lp[:, 1 + g * C1R:1 + (g + 1) * C1R], lay3(bank(g % 2, C1R * LPW), LPW),
                               ACT.Copy).then_inc(s_local_copied, 1)
            act.wait_ge(s_dw_taps, (im + 1) * T9)
            act.activation(UU, AC, ACT.Relu, bias=vec_of("three")).then_inc(s_local_relu3, 1)
            act.wait_ge(s_gate_logit, im + 1)
            act.activation(SM[:, 1:2], bank(2, 1), ACT.Sigmoid, bias=vec_of("gcb"),
                           scale=1.0 / (6 * KX * H)).then_inc(s_gate, 1)

        def c_dve(dve, im):
            dve.wait_ge(s_local_copied, (im + 1) * NC1)
            dve.wait_ge(s_borders_zeroed, (im + 1) * 3)
            a3 = lay3(AC, QY)
            for t in range(T9):
                src = lp[:, t % 3:t % 3 + KX, t // 3:t // 3 + QY]
                w = DW[:, t:t + 1]
                if t == 0:
                    dve.tensor_scalar(a3, src, w, None, ALU.mult).then_inc(s_dw_taps, 1)
                else:
                    dve.wait_ge(s_dw_taps, im * T9 + t)
                    dve.scalar_tensor_tensor(out=a3, in0=src, scalar=w, in1=a3, op0=ALU.mult,
                                             op1=ALU.add).then_inc(s_dw_taps, 1)
            dve.wait_ge(s_local_relu3, im + 1)
            dve.scalar_tensor_tensor(out=AC, in0=UU, scalar=6.0, in1=AC, op0=ALU.min, op1=ALU.mult).then_inc(s_local_swish, 1)
            dve.wait_ge(s_local_swish, im + 1)
            dve.tensor_reduce(SM[:, 0:1], AC, X, ALU.add).then_inc(s_local_sum, 1)
            dve.wait_ge(s_gate, im + 1)
            dve.tensor_scalar(AC, AC, SM[:, 1:2], 1.0 / 6, ALU.mult, ALU.mult).then_inc(s_local_gated, 1)

        def c_sync(sp, im):
            sp.wait_ge(s_local_gated, im + 1)
            for q in range(NQ):
                sp.dma_start(LOC[0:FG, q * KX * QY:(q + 1) * KX * QY], AC[q * FG:(q + 1) * FG, :]).then_inc(s_local_moved, 16)
            sp.dma_start(LOC[FG:FG + 1, :], ones).then_inc(s_local_moved, 16)

        NF = NQ * NK

        def at(n_g, n_q, lag):
            q = n_q - lag
            g = n_g + q // NQ
            q %= NQ
            return g, q, g * NQ + q

        def there(n_g, n_q, lag, full):
            return full or 0 <= n_g * NQ + n_q - lag < NF

        def d_pe(pe, im, g, q, full):
            if there(g, q, 0, full):
                _, _, n = at(g, q, 0)
                b = 3 * (q % 2)
                if full or n >= 2:
                    pe.wait_ge(s_filt_shifted, im * NF + n - 1)
                src = LOC.rearrange("p (q k) -> p q k", q=NQ)[:, q, bass.ds(g * FN, FN)]
                for t in range(T9):
                    i = pe.matmul(bank(b + t // 3, FN, (t % 3) * FN), HW[:, t * P:(t + 1) * P], src,
                                  start=(t % 3 == 0), stop=(t % 3 == 2), skip_group_check=True)
                i.then_inc(s_filt_logits, 1)
            if there(g, q, 3, full):
                _, _, n = at(g, q, 3)
                pe.wait_ge(s_filt_products_paired, im * NF + n + 1)
                if later(n, 2):
                    pe.wait_ge(s_filtered, im * NF + n - 1)
                for t in (0, 1, 4, 5, 6, 7, 8):
                    i = pe.matmul(bank(6 + (q - 3) % 2, FN), IDN, PD[(q - 3) % 4][:, t * FN:(t + 1) * FN],
                                  start=(t == 0), stop=(t == T9 - 1))
                i.then_inc(s_filt_weighted, 1)

        def d_dve(dve, im, g, q, full):
            if there(g, q, 0, full):
                _, _, n = at(g, q, 0)
                b = 3 * (q % 2)
                lg = PS[:, b:b + 3, 0:3 * FN].rearrange("p b (t n) -> p b t n", t=3)
                dve.wait_ge(s_filt_logits, im * NF + n + 1)
                dve.tensor_reduce(MXF[q % 2], lg.rearrange("p b t n -> p n b t"), mybir.AxisListType.XY,
                                  ALU.max).then_inc(s_filt_max, 1)
            if there(g, q, 1, full):
                _, _, n = at(g, q, 1)
                u = (q + 1) % 2
                dve.wait_ge(s_filt_exp, im * NF + n + 1)
                if later(n, 2):
                    dve.wait_ge(s_filt_sum_inv, im * NF + n - 1)
                dve.tensor_reduce(DEN[u], EE[u].rearrange("p (t n) -> p n t", t=T9), X, ALU.add).then_inc(s_filt_sum, 1)
            if there(g, q, 0, full):
                _, _, n = at(g, q, 0)
                dve.wait_ge(s_filt_max, im * NF + n + 1)
                if full or n >= 2:
                    dve.wait_ge(s_filt_products, im * NF + n - 1)
                    dve.wait_ge(s_filt_sum, im * NF + n - 1)
                mx = MXF[q % 2].unsqueeze(1).unsqueeze(1).broadcast_to([P, 3, 3, FN])
                dve.tensor_tensor(EE[q % 2].rearrange("p (b t n) -> p b t n", b=3, t=3), lg, mx,
                                  ALU.subtract).then_inc(s_filt_shifted, 1)
            if there(g, q, 3, full):
                gg, qq, n = at(g, q, 3)
                dve.wait_ge(s_filt_weighted, im * NF + n + 1)
                dve.wait_ge(s_filt_sum_inv, im * NF + n + 1)
                dst = lay3(FMP, H)[:, bass.ds(gg * KR, KR), qq * QY:(qq + 1) * QY]
                dve.tensor_tensor(dst, lay3(bank(6 + qq % 2, FN), QY), lay3(RDN[qq], QY), ALU.mult).then_inc(s_filtered, 1)

        def d_act(act, im, g, q, full):
            if there(g, q, 0, full):
                _, _, n = at(g, q, 0)
                act.wait_ge(s_filt_shifted, im * NF + n + 1)
                act.activation(EE[q % 2], EE[q % 2], ACT.Exp).then_inc(s_filt_exp, 1)
            if there(g, q, 1, full):
                _, _, n = at(g, q, 1)
                u = (q + 1) % 2
                act.wait_ge(s_filt_sum, im * NF + n + 1)
                r = (q - 1) % NQ
                if later(n, 4):
                    act.wait_ge(s_filtered, im * NF + n - 3)
                act.activation(RDN[r], DEN[u], ACT.Ln).then_inc(s_filt_ln, 1)
                act.wait_ge(s_filt_ln, im * NF + n + 1)
                act.activation(RDN[r], RDN[r], ACT.Exp, scale=-1.0).then_inc(s_filt_sum_inv, 1)

        def d_pool(pool, im, g, q, full):
            if there(g, q, 0, full):
                _, _, n = at(g, q, 0)
                pool.wait_ge(s_filt_exp, im * NF + n + 1)
                if full:
                    pool.wait_ge(s_filt_weighted, im * NF + n - 3)
                for i in range(3):
                    e = EE[q % 2].rearrange("p (i j k y) -> p i j k y", i=3, j=3, k=KR)[:, i]
                    d = PD[q].rearrange("p (i j k y) -> p i j k y", i=3, j=3, k=KR)[:, i]
                    win = mp[:, bass.ds(g * KR, KR), q * QY + i:q * QY + i + QY]
                    win = bass.AP(win.tensor, win.offset, [list(win.ap[0]), [MPW, 3]] + [list(a) for a in win.ap[1:]])
                    ins = pool.tensor_tensor(d, e, win, ALU.mult)
                ins.then_inc(s_filt_products, 1)
                pool.wait_ge(s_filt_products, im * NF + n + 1)
                pool.tensor_tensor(PD[q][:, 0:2 * FN], PD[q][:, 0:2 * FN], PD[q][:, 2 * FN:4 * FN],
                                   ALU.add).then_inc(s_filt_products_paired, 1)

        def filter_loop(eng, stage, im):
            for g in range(2):
                for q in range(NQ):
                    stage(eng, im, g, q, False)
            with eng.Fori(2, NK) as g:
                for q in range(NQ):
                    stage(eng, im, g, q, True)
            for q in range(3):
                stage(eng, im, NK, q, False)

        TG = [(0, 1)] + [(k, min(4, 32 - k)) for k in range(1, 32, 4)] + [(32, 1)]
        NT = 2 * len(TG)
        za, zb = (a.rearrange("p (c k) -> p c k", k=P) for a in (ZA, ZB))
        bfc = BF.rearrange("p (h s c) -> p s h c", h=H // 2, s=2)

        def e_sync(sp, im):
            sp.wait_ge(s_filtered, (im + 1) * NF)
            f = lay3(FMP, H)
            for src, dst in ((f[0:C], FM2), (f[C:P], FP2)):
                for g in range(2):
                    sp.dma_start(lay3(dst, H)[g * C:(g + 1) * C], src[:, 32 * g:32 * g + KG]).then_inc(s_filtered_moved, 16)

        def e_pe(pe, im):
            n = 0
            for made, src in ((s_im_made, SN), (s_re_made, CO)):
                pe.wait_ge(made, im + 1)
                for k0, m in TG:
                    if n >= 4:
                        pe.wait_ge(s_spec_copied[0], im * NT + n - 3)
                        pe.wait_ge(s_spec_copied[1], im * NT + n - 3)
                    for j in range(m):
                        i = pe.transpose(bank(n % 4, P, j * P), src[:, (k0 + j) * H:(k0 + j + 1) * H], IDN)
                    i.then_inc(s_spec_transposed, 1)
                    n += 1
            pe.wait_ge(s_spec_copied[0], (im + 1) * NT)
            pe.wait_ge(s_spec_copied[1], (im + 1) * NT)
            for g in range(C // 4):
                if g >= 4:
                    pe.wait_ge(s_idft_h_copied[g % 2], im * (C // 8) + (g - 4) // 2 + 1)
                for j in range(4):
                    c = 4 * g + j
                    pe.matmul(bank(g % 4, H, j * H), za[:, c], ICS[:, 0:H], start=(j == 0), stop=False,
                              skip_group_check=True)
                    i = pe.matmul(bank(g % 4, H, j * H), zb[:, c], ICS[:, H:2 * H], start=False, stop=(j == 3),
                                  skip_group_check=True)
                i.then_inc(s_idft_h_made, 1)
            pe.wait_ge(s_idft_h_copied[0], (im + 1) * (C // 8))
            pe.wait_ge(s_idft_h_copied[1], (im + 1) * (C // 8))
            for k in range(NCH):
                if k >= 4:
                    pe.wait_ge(s_x2_done, im * NCH + k - 3)
                for r in range(RPC):
                    h = RPC * k + r
                    i = pe.matmul(bank(k % 4, W, r * W), BF[:, h * P:(h + 1) * P], IFW,
                                  start=(r == 0), stop=(r == RPC - 1), skip_group_check=True)
                i.then_inc(s_idft_w_made, 1)

        def e_zcopy(im, me, eng, n, real, k0, m, emit):
            src = bank(n % 4, m * P).rearrange("p (t g c) -> p g c t", t=m, g=2)
            first = (real and me == 0) or (not real and me == 1)
            off = k0 if first else 64 + k0
            todo = []
            for g in range(2):
                if not first and ((k0 == 0 and g == 0) or (k0 == 32 and g == 1)):
                    continue
                todo.append(((za, zb)[me][:, :, off + 32 * g:off + 32 * g + m], src[:, g]))
            for j, (dst, sr) in enumerate(todo):
                i = emit(dst, sr, real)
            i.then_inc(s_spec_copied[me], 1)

        def e_act(act, im):
            act.wait_ge(s_angle_clamped, im + 1)
            act.activation(SN, FP2, ACT.Sin).then_inc(s_sin_made, 1)
            act.activation(CO, FP2, ACT.Abs).then_inc(s_angle_abs, 1)
            act.wait_ge(s_angle_abs, im + 1)
            act.activation(CO, CO, ACT.Sin, bias=vec_of("half_pi"), scale=-1.0).then_inc(s_cos_made, 1)
            n = 0
            for real in (False, True):
                for k0, m in TG:
                    act.wait_ge(s_spec_transposed, im * NT + n + 1)
                    if n % 2:
                        act.wait_ge(s_spec_copied[1], im * NT + n + 1)
                    e_zcopy(im, 0, act, n, real, k0, m, lambda o_, i_, r_: act.activation(o_, i_, ACT.Copy))
                    n += 1
            for g in range(0, C // 4, 2):
                act.wait_ge(s_idft_h_made, im * (C // 4) + g + 1)
                act.activation(bfc[:, :, :, 4 * g:4 * g + 4], bank(g % 4).rearrange("p (c s h) -> p s h c", c=4, s=2),
                               ACT.Copy).then_inc(s_idft_h_copied[0], 1)

        def e_dve(dve, im):
            dve.wait_ge(s_filtered_moved, (im + 1) * 64)
            dve.tensor_scalar(FP2, FP2, PI, -PI, ALU.min, ALU.max).then_inc(s_angle_clamped, 1)
            dve.wait_ge(s_cos_made, im + 1)
            dve.tensor_tensor(CO, CO, FM2, ALU.mult).then_inc(s_re_made, 1)
            n = 0
            for real in (False, True):
                for k0, m in TG:
                    dve.wait_ge(s_spec_transposed, im * NT + n + 1)
                    if n % 2 == 0:
                        dve.wait_ge(s_spec_copied[0], im * NT + n + 1)
                    e_zcopy(im, 1, dve, n, real, k0, m,
                            lambda o_, i_, r_: dve.tensor_copy(o_, i_) if r_ else
                            dve.tensor_scalar(o_, i_, -1.0, None, ALU.mult))
                    n += 1
            for g in range(1, C // 4, 2):
                dve.wait_ge(s_idft_h_made, im * (C // 4) + g + 1)
                dve.tensor_copy(bfc[:, :, :, 4 * g:4 * g + 4], bank(g % 4).rearrange("p (c s h) -> p s h c", c=4, s=2)).then_inc(s_idft_h_copied[1], 1)
            for k in range(NCH):
                dve.wait_ge(s_idft_w_made, im * NCH + k + 1)
                dve.tensor_tensor(XC[:, k * CH:(k + 1) * CH], XC[:, k * CH:(k + 1) * CH], bank(k % 4),
                                  ALU.add).then_inc(s_x2_done, 1)
            dve.memset(xpv[:, 0:H + 2:H + 1, :], 0.0).then_inc(s_image_borders_zeroed, 1)
            dve.memset(xpv[:, 1:H + 1, 0:XPW:XPW - 1], 0.0).then_inc(s_image_borders_zeroed, 1)

        def e_pool(pool, im):
            pool.wait_ge(s_sin_made, im + 1)
            pool.wait_ge(s_filtered_moved, (im + 1) * 64)
            pool.tensor_tensor(SN, SN, FM2, ALU.mult).then_inc(s_im_made, 1)

        def convs(k):
            if isinstance(k, int):
                first = [(max(2 * k - 7, 0), k - 3)] if 3 <= k <= NCH + 2 else []
                second = [(2 * k - 6, k + 13)] if 4 <= k <= NCH + 2 else []
                return first, second
            return [(k * 2 - 7, k - 3)], [(k * 2 - 6, k + 13)]

        def first_bank(m, u):
            return 0 if isinstance(m, int) and m == 0 else (2 * u - 7) % 4

        def f_pe(pe, im):
            def conv(m, mu, y):
                if later(m, 4):
                    pe.wait_ge(s_hidden_done, im * NY + m - 3)
                for j in range(3):
                    pe.matmul(bank(2 + mu % 4), CWP[:, j * P:(j + 1) * P], xpv[:, bass.ds(y * 4, 4), j:j + W],
                              start=(j == 0), stop=False)
                for j in range(3):
                    i = pe.matmul(bank(2 + mu % 4), CWS[:, j * P:(j + 1) * P], xpv[0:C, bass.ds(y * 4 + 2, 4), j:j + W],
                                  start=False, stop=(j == 2))
                i.then_inc(s_conv_made, 1)

            def step(k, u, rnd):
                norm = not isinstance(k, int) or k < NCH
                first, second = convs(k)
                if norm:
                    pe.wait_ge(s_x2_done, (im + 1) * NCH)
                    if later(k):
                        pe.wait_ge(s_scaled4, im * NCH + k)
                    pe.matmul(bank(0), CEN, XC[:, bass.ds(k * CH, CH)], start=True, stop=True).then_inc(s_centred4, 1)
                for m, y in first:
                    if isinstance(k, int) and k == 3:
                        pe.wait_ge(s_image_borders_zeroed, (im + 1) * 2)
                        pe.wait_ge(s_rows_moved[0], (im * (NCH // 4) + 1) * 64)
                    if norm or k <= NCH + 1:
                        r = rnd - 1 if u < 2 else rnd
                        pe.wait_ge(s_rows_moved[(u - 2) % 4], (im * (NCH // 4) + r + 1) * 64)
                    conv(m, first_bank(m, u), y)
                if norm:
                    pe.wait_ge(s_square4, im * NCH + k + 1)
                    pe.matmul(bank(1), ONE, SQE, start=True, stop=True).then_inc(s_var4, 1)
                for m, y in second:
                    conv(m, (2 * u - 6) % 4, y)
            for k in range(8):
                step(k, k % 4, k // 4)
            with pe.Fori(2, NCH // 4) as k4:
                for u in range(4):
                    step(k4 * 4 + u, u, k4)
            for k in range(NCH, NCH + 3):
                step(k, k % 4, k // 4)
            conv(NY - 1, NY - 1, NCH)

            pe.wait_ge(s_hidden_sum, im + 1)
            pe.matmul(bank(6, 1)[0:FG], SE1[:, :], SM[:, 2:3], start=True, stop=True).then_inc(s_se1_made, 1)
            pe.wait_ge(s_se1_relu, im + 1)
            pe.matmul(bank(6, 1, 8), SE2[:, :], SM[0:FG, 3:4], start=True, stop=True).then_inc(s_se2_made, 1)
            pe.wait_ge(s_w_out_scaled, im + 1)

            def project(k, u):
                for h in range(2):
                    i = pe.matmul(bank(u), WS[:, h * P:(h + 1) * P], HID[:, bass.ds(k * CH + h * (H * W // 2), CH)],
                                  start=(h == 0), stop=(h == 1))
                i.then_inc(s_projected, 1)
            project(0, 0)
            project(1, 1)
            with pe.Fori(1, NCH // 2) as k2:
                for u in range(2):
                    pe.wait_ge(s_out_ready, im * NCH + k2 * 2 + u - 1)
                    project(k2 * 2 + u, u)

        def f_act(act, im):
            def relu3(m, mu):
                act.wait_ge(s_conv_made, im * NY + m + 1)
                if later(m, 2):
                    act.wait_ge(s_hidden_done, im * NY + m - 1)
                act.activation(UE[mu % 2], bank(2 + mu % 4), ACT.Relu, bias=vec_of("three")).then_inc(s_conv_relu3, 1)

            def step(k, u, rnd):
                norm = not isinstance(k, int) or k < NCH
                first, second = convs(k)
                if norm:
                    act.wait_ge(s_centred4, im * NCH + k + 1)
                    act.activation(SQE, bank(0), ACT.Square).then_inc(s_square4, 1)
                for m, y in first:
                    relu3(m, first_bank(m, u))
                if norm:
                    act.wait_ge(s_var4, im * NCH + k + 1)
                    act.activation(RSE, bank(1), ACT.Ln, bias=vec_of("eps")).then_inc(s_ln4, 1)
                    act.wait_ge(s_ln4, im * NCH + k + 1)
                    act.activation(RSE, RSE, ACT.Exp, scale=-0.5).then_inc(s_rstd4, 1)
                    act.wait_ge(s_scaled4, im * NCH + k + 1)
                    if later(k, 2):
                        r = rnd - 1 if u < 2 else rnd
                        act.wait_ge(s_rows_moved[(u - 2) % 4], (im * (NCH // 4) + r + 1) * 64)
                    act.activation(XNE[u % 2], XHE, ACT.Identity, bias=vec_of("n2b")).then_inc(s_normed4, 1)
                for m, y in second:
                    relu3(m, (2 * u - 6) % 4)
            for k in range(8):
                step(k, k % 4, k // 4)
            with act.Fori(2, NCH // 4) as k4:
                for u in range(4):
                    step(k4 * 4 + u, u, k4)
            for k in range(NCH, NCH + 3):
                step(k, k % 4, k // 4)
            relu3(NY - 1, NY - 1)
            act.wait_ge(s_se1_made, im + 1)
            act.activation(SM[0:FG, 3:4], bank(6, 1)[0:FG], ACT.Relu, bias=vec_of("se1b", FG),
                           scale=1.0 / (6 * H * W)).then_inc(s_se1_relu, 1)
            act.wait_ge(s_se2_made, im + 1)
            act.activation(SM[:, 4:5], bank(6, 1, 8), ACT.Relu, bias=vec_of("se2b3")).then_inc(s_se2_relu, 1)

        def f_dve(dve, im):
            def swish(m, mu, y):
                dve.wait_ge(s_conv_relu3, im * NY + m + 1)
                dve.scalar_tensor_tensor(out=HID[:, bass.ds(y * CH, CH)], in0=UE[mu % 2], scalar=6.0,
                                         in1=bank(2 + mu % 4), op0=ALU.min, op1=ALU.mult,
                                         accum_out=SM[:, bass.ds(m + 8, 1)]).then_inc(s_hidden_done, 1)

            def step(k, u):
                norm = not isinstance(k, int) or k < NCH
                first, second = convs(k)
                for m, y in first:
                    swish(m, first_bank(m, u), y)
                if norm:
                    dve.wait_ge(s_rstd4, im * NCH + k + 1)
                    if later(k):
                        dve.wait_ge(s_normed4, im * NCH + k)
                    dve.scalar_tensor_tensor(out=XHE, in0=bank(0), scalar=vec_of("n2g"), in1=RSE, op0=ALU.mult,
                                             op1=ALU.mult).then_inc(s_scaled4, 1)
                for m, y in second:
                    swish(m, (2 * u - 6) % 4, y)
            for k in range(8):
                step(k, k % 4)
            with dve.Fori(2, NCH // 4) as k4:
                for u in range(4):
                    step(k4 * 4 + u, u)
            for k in range(NCH, NCH + 3):
                step(k, k % 4)
            swish(NY - 1, NY - 1, NCH)
            dve.wait_ge(s_hidden_done, (im + 1) * NY)
            dve.tensor_reduce(SM[:, 2:3], SUMH, X, ALU.add).then_inc(s_hidden_sum, 1)
            dve.wait_ge(s_se2_relu, im + 1)
            dve.tensor_scalar(SM[:, 5:6], SM[:, 4:5], 6.0, 1.0 / 36, ALU.min, ALU.mult).then_inc(s_se_gate, 1)
            dve.wait_ge(s_se_gate, im + 1)
            dve.tensor_scalar(WS[:, :], WF[:, :], SM[:, 5:6], None, ALU.mult).then_inc(s_w_out_scaled, 1)

            def add_out(k, u, j=0):
                dve.wait_ge(s_projected, im * NCH + k + 1)
                if not isinstance(k, int):
                    dve.wait_ge(s_written[u], (im * (NCH // 2) + j) * 32)
                dve.scalar_tensor_tensor(out=OB[u], in0=bank(u), scalar=vec_of("ob"),
                                         in1=XC[:, bass.ds(k * CH, CH)], op0=ALU.add, op1=ALU.add).then_inc(s_out_ready, 1)
            add_out(0, 0)
            add_out(1, 1)
            with dve.Fori(1, NCH // 2) as k2:
                for u in range(2):
                    add_out(k2 * 2 + u, u, k2)

        def f_sync(sp, im, more):
            with sp.Fori(0, NCH // 4) as k4:
                for u in range(4):
                    k = k4 * 4 + u
                    sp.wait_ge(s_image_borders_zeroed, (im + 1) * 2)
                    sp.wait_ge(s_normed4, im * NCH + k + 1)
                    for h in range(2):
                        src = lay3(XNE[u % 2][h * C:(h + 1) * C], W)
                        r0 = k * RPC + h * (H // 2)
                        sp.dma_start(xpv[0:C, bass.ds(r0 + 1, RPC), 1:1 + W], src).then_inc(s_rows_moved[u], 16)
                        sp.dma_start(xpv[C:P, bass.ds(r0, RPC), 1:1 + W], src).then_inc(s_rows_moved[u], 16)
            xo = out.rearrange("b c (s h) w -> b s c (h w)", s=2)
            def store(k, u):
                sp.wait_ge(s_out_ready, im * NCH + k + 1)
                for h in range(2):
                    sp.dma_start(xo[bass.ds(im, 1), h, :, bass.ds(k * CH, CH)].squeeze(0),
                                 OB[u][h * C:(h + 1) * C]).then_inc(s_written[u], 16)
            with sp.Fori(0, NCH // 2 - 1) as k2:
                for u in range(2):
                    store(k2 * 2 + u, u)
                if more:
                    x_load(sp, im + 1, k2)
            for u in range(2):
                store(NCH - 2 + u, u)
            for u in range(2):
                sp.wait_ge(s_written[u], (im + 1) * (NCH * 16))
            if more:
                x_load(sp, im + 1, NCH // 2 - 1)

        xi = x.rearrange("b c (s h) w -> b s c (h w)", s=2)

        def x_load(sp, im, j):
            for h in range(2):
                sp.dma_start(XC[h * C:(h + 1) * C, bass.ds(j * 2 * CH, 2 * CH)],
                             xi[bass.ds(im, 1), h, :, bass.ds(j * 2 * CH, 2 * CH)].squeeze(0)).then_inc(s_x_loaded, 16)

        def load_set(act, n):
            tables[0] += 1
            act.add_instruction(mybir.InstLoadActFuncSet(
                name=f"I-{900000 + tables[0]}", act_func_set_id=n, engine=mybir.EngineType.Activation,
                ins=[], outs=[]))
        tables = [0]

        def weight_loads():
            yield TB[:, :], tabs
            yield V[:, 0:NLOADED], vec
            wq = WQ[:, :].rearrange("p (j s c) -> p j s c", j=3, s=2)
            for h in range(2):
                r = slice(h * C, (h + 1) * C)
                yield wq[r, :, h], wqkv
                yield WO[r, r], wo
                yield W1[r, r], f1t
                yield WN[r, r], f2
                yield W1D[r, :], w1t
                yield WF[:, h * P + h * C:h * P + (h + 1) * C], w2t
            for q in range(NQ):
                yield LW[:, q * P + q * FG:q * P + (q + 1) * FG], l1t
                yield DW[q * FG:(q + 1) * FG, :], dwt
                for q2 in range(NQ):
                    yield GC[q * FG:(q + 1) * FG, q2 * FG:(q2 + 1) * FG], gct
            yield HW[0:FG, :], head
            yield HW[FG:FG + 1, :], head_b
            yield D9[:, :], d9.partition_broadcast(P)
            yield SE1[:, :], se1t
            yield SE2[:, :], se2t
        N_W = len(list(weight_loads())) * 16

        block = ctx.enter_context(nc.Block())

        @block.sync
        def _(sp):
            sp.wait_ge(s_weights_zeroed, 7)
            for dst, src in weight_loads():
                sp.dma_start(dst, src).then_inc(s_weights_loaded, 16)
            sp.wait_ge(s_weights_made, 12)
            with sp.Fori(0, NCH // 2) as j:
                x_load(sp, 0, j)

            def image(im, more):
                b_sync(sp, im)
                c_sync(sp, im)
                e_sync(sp, im)
                f_sync(sp, im, more)
            if n_img > 1:
                with sp.Fori(0, n_img - 1) as im:
                    image(im, True)
            image(n_img - 1, False)
            for u in range(2):
                sp.wait_ge(s_written[u], n_img * NCH * 16)

        @block.gpsimd
        def _(pool):
            for t in (WQ, WO, W1, LW, WF, HW):
                pool.memset(t[:, :], 0.0).then_inc(s_weights_zeroed, 1)
            pool.memset(WN, 0.0).then_inc(s_weights_zeroed, 1)
            for i, v in enumerate((1e-5, HALF_PI, 3.0, 1e-8, 2 * HALF_PI)):
                pool.memset(V[:, NLOADED + i:NLOADED + i + 1], v).then_inc(s_vec_constants, 1)
            with pool.Fori(0, n_img) as im:
                pipeline(pool, a_pool, im)
                b_pool(pool, im)
                filter_loop(pool, d_pool, im)
                e_pool(pool, im)

        @block.tensor
        def _(pe):
            pe.wait_ge(s_weights_loaded, N_W)
            pe.matmul(bank(0, P), WN, CEN, start=True, stop=True)
            pe.matmul(bank(0, 1, P), CEN, vec_of("f2b"), start=True, stop=True).then_inc(s_ffn2_folded, 1)
            pe.wait_ge(s_weights_made, 12)
            with pe.Fori(0, n_img) as im:
                pipeline(pe, a_pe, im)
                b_pe(pe, im)
                c_pe(pe, im)
                pe.wait_ge(s_local_moved, (im + 1) * 80)
                filter_loop(pe, d_pe, im)
                e_pe(pe, im)
                f_pe(pe, im)

        @block.scalar
        def _(act):
            act.wait_ge(s_weights_loaded, N_W)
            act.wait_ge(s_vec_constants, 5)
            act.wait_ge(s_weights_made, 12)
            with act.Fori(0, n_img) as im:
                load_set(act, SET_LN_EXP)
                pipeline(act, a_act, im)
                b_act(act, im)
                c_act(act, im)
                load_set(act, SET_LN_EXP)
                filter_loop(act, d_act, im)
                e_act(act, im)
                load_set(act, SET_LN_EXP)
                f_act(act, im)

        @block.vector
        def _(dve):
            dve.wait_ge(s_weights_loaded, N_W)
            dve.wait_ge(s_vec_constants, 5)
            for j in range(3):
                for i in range(3):
                    dst = CWS if i == 2 else CWP
                    lo = C * (i == 1)
                    t = 3 * i + j
                    dve.tensor_tensor(dst[lo:lo + C, j * P:(j + 1) * P], W1D[lo:lo + C], D9[lo:lo + C, t * P:(t + 1) * P],
                                      ALU.mult).then_inc(s_weights_made, 1)
            dve.tensor_scalar(vec_of("se2b3"), vec_of("se2b"), 3.0, None, ALU.add).then_inc(s_weights_made, 1)
            dve.wait_ge(s_ffn2_folded, 1)
            dve.tensor_copy(W2[:, :], bank(0, P)).then_inc(s_weights_made, 1)
            dve.tensor_copy(vec_of("f2c"), bank(0, 1, P)).then_inc(s_weights_made, 1)
            with dve.Fori(0, n_img) as im:
                pipeline(dve, a_dve, im)
                b_dve(dve, im)
                c_dve(dve, im)
                filter_loop(dve, d_dve, im)
                e_dve(dve, im)
                f_dve(dve, im)


def _tables():
    import numpy as np
    n = np.arange(P)
    blk = (n[:, None] // C == n[None, :] // C) / C
    k = np.arange(KX)

    def trig(a, b, f):
        m = np.outer(a, b) % P
        t = f(2 * np.pi * np.arange(P) / P)
        t[np.abs(t) < 1e-12] = 0
        return t[m]
    cw, sw = trig(n, k, np.cos), trig(n, k, np.sin)
    ch, sh = trig(n, n, np.cos), trig(n, n, np.sin)
    mult = np.where((k == 0) | (k == KX - 1), 1.0, 2.0)[:, None]
    inv = np.concatenate([mult * cw.T, (-2.0 * sw.T)[1:KX - 1]], 0) / P
    return np.concatenate([np.eye(P), np.eye(P) - blk, blk, cw / P, -sw / P, ch, -sh, sh, ch, ch, sh, inv],
                          1).astype(np.float32)


def kernel(**inputs):
    import numpy as np
    import concourse.bacc as bacc
    from concourse.bass_utils import run_bass_kernel_spmd

    a = {k: np.asarray(v) for k, v in inputs.items()}
    l0 = lambda n: a["L0_conv_" + n]
    l1 = lambda n: a["L1_conv_" + n]
    twice = lambda v: np.tile(v, 2)
    vec = np.stack([twice(l0("g1")), twice(l0("b1")), twice(l0("ffn1_b")), twice(l0("ffn2_b")), twice(l0("g2")),
                    twice(l0("b2")), twice(l1("norm1_g")), twice(l1("norm1_b")), twice(l1("norm2_g")),
                    twice(l1("norm2_b")), twice(l1("ffn2_b")), np.tile(l1("fgn_gc_b"), NQ), l1("se2_b"),
                    np.tile(l1("se1_b"), NQ)], 1)
    arrays = {
        "x": a["x"],
        "vec": vec,
        "tabs": _tables(),
        "wqkv": np.stack([l0(n).reshape(C, C) for n in ("W_Q", "W_K", "W_V")], 1),
        "wo": l0("W_O"),
        "f1t": l0("ffn1_w").T,
        "f2": l0("ffn2_w"),
        "l1t": l1("fgn_l1_w").T,
        "dwt": l1("fgn_dw_w").reshape(FG, T9),
        "gct": l1("fgn_gc_w").T,
        "head": l1("fgn_head_w").reshape(2, C, T9, FG).transpose(3, 2, 0, 1).reshape(FG, T9 * P),
        "head_b": l1("fgn_head_b").reshape(2, C, T9).transpose(2, 0, 1).reshape(1, T9 * P),
        "w1t": l1("ffn1_w").T,
        "d9": l1("ffn_dw_w").reshape(P, T9).T.reshape(T9 * P),
        "se1t": l1("se1_w").T,
        "se2t": l1("se2_w").T,
        "w2t": l1("ffn2_w").T,
        "ones": np.ones((1, NQ * KX * QY), np.float32),
    }
    arrays = {k + "_dram": np.ascontiguousarray(v) for k, v in arrays.items()}
    nc = bacc.Bacc("TRN2", target_bir_lowering=False, num_devices=1)
    args = [nc.dram_tensor(k, v.shape, mybir.dt.from_np(v.dtype), kind="ExternalInput").ap() for k, v in arrays.items()]
    out = nc.dram_tensor("out_dram", a["x"].shape, F32, kind="ExternalOutput").ap()
    build(nc, *args, out)
    r = run_bass_kernel_spmd(nc, [arrays], core_ids=[0])
    return r.results[0]["out_dram"]
```

```python
from contextlib import ExitStack

import concourse.bass as bass
from concourse import mybir

F32 = mybir.dt.float32
F32R = mybir.dt.float32r
ALU = mybir.AluOpType
ACT = mybir.ActivationFunctionType
X = mybir.AxisListType.X

P = 128
C = 64
H = W = 128
KX = W // 2 + 1
KG = 33
NH, HD = 8, 8
RPC = 4
CH = RPC * W
NCH = (H // 2) // RPC
NY = 32
FG = 32
NQ = 4
QY = H // NQ
KR = 5
NK = KX // KR
FN = KR * QY
T9 = 9
PI = 3.1415925025939941
HALF_PI = 1.5707963267948966
TINY = 1e-30
SET_LN_EXP = 6
SET_SIGMOID = 2

HEAD_W1H2, HEAD_B1, HEAD_B2, HEAD_W1H1, HEAD_W2H1 = 0, FG, FG + 1, 2 * FG, 3 * FG
HEAD_GROUPS = (HEAD_W1H2, HEAD_W1H1, HEAD_W2H1)

VECS = ["g1", "b1", "f1b", "f2b", "g2", "b2", "n1g", "n1b", "n2g", "n2b", "ob", "gcb", "se2b",
        "se1b", "gate_mul", "gate_add", "minus_b2", "eps", "half_pi", "three", "tiny_mag", "tiny", "minus4", "se2b3", "f2c"]
NLOADED = VECS.index("eps")


def build(nc, x, vec, tabs, wqkv, wo, f1t, f2, l1t, dwt, gct, head, head_b, w1t, d9, se1t, se2t, w2t, ones, out):
    n_img = x.shape[0]
    ctx = ExitStack()
    with ctx:
        def sb(name, n, parts=P, dtype=F32):
            return ctx.enter_context(nc.sbuf_tensor(name, [parts, n], dtype))

        def sem(name):
            return ctx.enter_context(nc.semaphore(name))

        TB = sb("tables", 3 * P + 130 + 3 * 256 + P)
        o = [0]

        def tab(n):
            o[0] += n
            return TB[:, o[0] - n:o[0]]
        IDN, CEN, ONE = tab(P), tab(P), tab(P)
        DFTW = tab(130)
        DRE, DIM = tab(256), tab(256)
        ICS = tab(256)
        IFW = tab(P)
        V = sb("vectors", len(VECS))
        WQ = sb("w_qkv", 3 * 2 * C)
        WO = sb("w_o", P)
        W1 = sb("w_ffn1", P)
        W2 = sb("w_ffn2", P)
        LW = sb("w_local", NQ * P)
        DW = sb("w_dw", T9)
        GC = sb("w_gate", P)
        HW = sb("w_head", T9 * P)
        NEGI = sb("neg_identity", P, dtype=F32R)
        CW1 = sb("w_conv1", T9 * P, dtype=F32R)
        CW2 = sb("w_conv2", T9 * P, dtype=F32R)
        PR = sb("parts", T9 * P + 2 * FN + 4 * FN, dtype=F32R)
        SE1 = sb("w_se1", FG)
        SE2 = sb("w_se2", P, FG)
        WF = sb("w_out", 2 * P)
        SM = sb("small", 64)
        XC = sb("x_chan", NCH * CH)
        AR = sb("arena", 35844)
        PS = ctx.enter_context(nc.psum_tensor("ps", [P, 8, 512], F32))

        def vec_of(name, parts=P):
            i = VECS.index(name)
            return V[0:parts, i:i + 1]

        def area(off, n):
            return AR[:, off:off + n]

        XP1 = area(0, 8192)
        o[0] = 8192

        def part(n):
            o[0] += n
            return area(o[0] - n, n)
        PROD = part(RPC * 2 * 512)
        PV = [part(RPC * 2 * 512) for _ in range(2)]
        QS = [part(RPC * 384) for _ in range(2)]
        XN = [part(CH) for _ in range(4)]
        SC, EX, PB, OS, Y0, Y1 = (part(CH) for _ in range(6))
        SQ = [part(CH) for _ in range(3)]
        RS = [part(CH) for _ in range(3)]
        XH = [part(CH) for _ in range(3)]
        XT = part(CH)
        MX, SU, RI = part(C), part(C), part(C)
        AF = area(8192, 2 * KG * P)
        RE, IM, MG, TT = (area(16640 + i * KG * H, KG * H) for i in range(4))
        MPW = H + 2
        MP = area(0, (KX + 2) * MPW)
        LPW = QY + 2
        LP = area(8710, (KX + 2) * LPW)
        AT = [[area(o_ + 448 * i, 448) for i in range(3)] for o_ in (10988, 15148)]
        AC, UU = area(31200, KX * QY), area(13068, KX * QY)
        LOC = area(16640, NQ * KX * QY)
        HWG = PR[:, 0:T9 * P]
        MXF = [PR[:, T9 * P + i * FN:T9 * P + (i + 1) * FN] for i in range(2)]
        LOCP = [PR[:, T9 * P + (2 + i) * FN:T9 * P + (3 + i) * FN] for i in range(4)]
        FMP = area(24960, KX * H)
        PD = [area(8710 + i * T9 * FN, T9 * FN) for i in range(4)]
        EE = [area(14470, T9 * FN), area(33280, T9 * FN)]
        DEN = [area(15910 + i * FN, FN) for i in range(2)]
        RDN = [area(34720 + i * FN, FN) for i in range(4)]
        LSUM, GMUL = SM[:, 40:45], SM[:, 45:46]
        FP2, FM2 = area(0, KG * H), area(KG * H, KG * H)
        SN, CO = area(8448, KG * H), area(12672, KG * H)
        ZA, ZB = area(16896, C * P), area(25088, C * P)
        BF = area(0, C * P)
        XPW = W + 2
        XP = area(0, (H + 2) * XPW)
        HID = area(16900, H * W)
        o[0] = 33284
        SQE = part(CH)
        RSE = SQE
        XNE = [part(CH) for _ in range(2)]
        XW = [PR[:, i * 6 * XPW:(i + 1) * 6 * XPW] for i in range(2)]
        UE = [part(CH) for _ in range(2)]
        OB = [area(i * CH, CH) for i in range(4)]
        WS = area(4 * CH, 2 * P)
        SUMH = SM[:, 8:8 + NY]
        D9 = area(0, T9 * P)
        W9 = area(T9 * P, T9 * P)
        W1D = area(2 * T9 * P, P)
        WN = area((2 * T9 + 1) * P, P)

        s_scaled1 = sem("s_scaled1")
        s_centred1 = sem("s_centred1")
        s_attn_relu = sem("s_attn_relu")
        s_ffn1_made = sem("s_ffn1_made")
        s_normed3 = sem("s_normed3")
        s_ffn1_relu = sem("s_ffn1_relu")
        s_transposed = sem("s_transposed")
        s_square1 = sem("s_square1")
        s_var1 = sem("s_var1")
        s_scaled2 = sem("s_scaled2")
        s_ffn2_centred = sem("s_ffn2_centred")
        s_square2 = sem("s_square2")
        s_scaled3 = sem("s_scaled3")
        s_var2 = sem("s_var2")
        s_normed1 = sem("s_normed1")
        s_qkv_copied = sem("s_qkv_copied")
        s_qkv_made = sem("s_qkv_made")
        s_pv_halved = sem("s_pv_halved")
        s_attn_copied = sem("s_attn_copied")
        s_layer0_out = sem("s_layer0_out")
        s_centred3 = sem("s_centred3")
        s_attn_summed = sem("s_attn_summed")
        s_square3 = sem("s_square3")
        s_var3 = sem("s_var3")
        s_pixels_copied = sem("s_pixels_copied")
        s_attn_projected = sem("s_attn_projected")
        s_ln1 = sem("s_ln1")
        s_rstd1 = sem("s_rstd1")
        s_ln2 = sem("s_ln2")
        s_rstd2 = sem("s_rstd2")
        s_scores_shifted = sem("s_scores_shifted")
        s_score_exp = sem("s_score_exp")
        s_pv_products = sem("s_pv_products")
        s_residual_added = sem("s_residual_added")
        s_ln3 = sem("s_ln3")
        s_rstd3 = sem("s_rstd3")
        s_qk_products = sem("s_qk_products")
        s_scores = sem("s_scores")
        s_score_max = sem("s_score_max")
        s_exp_sum = sem("s_exp_sum")
        s_exp_sum_inv = sem("s_exp_sum_inv")
        s_probs = sem("s_probs")
        s_dft_w_made = sem("s_dft_w_made")
        s_dft_h_made = sem("s_dft_h_made")
        s_mag_squared = sem("s_mag_squared")
        s_re_copied = sem("s_re_copied")
        s_im_copied = sem("s_im_copied")
        s_re_square = sem("s_re_square")
        s_im_square = sem("s_im_square")
        s_im_square_last = sem("s_im_square_last")
        s_mag_ln = sem("s_mag_ln")
        s_mag = sem("s_mag")
        s_im_abs = sem("s_im_abs")
        s_phase_den_ln = sem("s_phase_den_ln")
        s_im_factor = sem("s_im_factor")
        s_phase_den = sem("s_phase_den")
        s_mag_done = sem("s_mag_done")
        s_half_tan = sem("s_half_tan")
        s_half_angle = sem("s_half_angle")
        s_phase_den_inv = sem("s_phase_den_inv")
        s_im_sign = sem("s_im_sign")
        s_borders_zeroed = sem("s_borders_zeroed")
        s_phase_done = sem("s_phase_done")
        s_local_copied = sem("s_local_copied")
        s_local_made = sem("s_local_made")
        s_local_sum = sem("s_local_sum")
        s_gate_logit = sem("s_gate_logit")
        s_dw_taps = sem("s_dw_taps")
        s_act_taps = sem("s_act_taps")
        s_taps_paired = sem("s_taps_paired")
        s_taps_summed = sem("s_taps_summed")
        s_local_relu3 = sem("s_local_relu3")
        s_gate = sem("s_gate")
        s_local_swish = sem("s_local_swish")
        s_head_in_part1 = sem("s_head_in_part1")
        s_head_in_made = sem("s_head_in_made")
        s_rows_part1 = sem("s_rows_part1")
        s_rows_made = sem("s_rows_made")
        s_gate_factor = sem("s_gate_factor")
        s_head_part1 = sem("s_head_part1")
        s_head_gated = sem("s_head_gated")
        s_filt_logits = sem("s_filt_logits")
        s_filt_shifted = sem("s_filt_shifted")
        s_filtered = sem("s_filtered")
        s_filt_weighted = sem("s_filt_weighted")
        s_filt_max = sem("s_filt_max")
        s_filt_exp = sem("s_filt_exp")
        s_filt_sum_inv = sem("s_filt_sum_inv")
        s_filt_sum = sem("s_filt_sum")
        s_filt_products = sem("s_filt_products")
        s_filt_ln = sem("s_filt_ln")
        s_spec_transposed = sem("s_spec_transposed")
        s_idft_h_made = sem("s_idft_h_made")
        s_x2_done = sem("s_x2_done")
        s_idft_w_made = sem("s_idft_w_made")
        s_angle_clamped = sem("s_angle_clamped")
        s_sin_made = sem("s_sin_made")
        s_angle_abs = sem("s_angle_abs")
        s_cos_made = sem("s_cos_made")
        s_image_borders_zeroed = sem("s_image_borders_zeroed")
        s_hidden_done = sem("s_hidden_done")
        s_conv_made = sem("s_conv_made")
        s_scaled4 = sem("s_scaled4")
        s_centred4 = sem("s_centred4")
        s_square4 = sem("s_square4")
        s_var4 = sem("s_var4")
        s_hidden_sum = sem("s_hidden_sum")
        s_se1_made = sem("s_se1_made")
        s_se1_relu = sem("s_se1_relu")
        s_se2_made = sem("s_se2_made")
        s_w_out_scaled = sem("s_w_out_scaled")
        s_projected = sem("s_projected")
        s_out_ready = sem("s_out_ready")
        s_conv_relu3 = sem("s_conv_relu3")
        s_ln4 = sem("s_ln4")
        s_rstd4 = sem("s_rstd4")
        s_normed4 = sem("s_normed4")
        s_se2_relu = sem("s_se2_relu")
        s_se_gate = sem("s_se_gate")
        s_weights_zeroed = sem("s_weights_zeroed")
        s_weights_loaded = sem("s_weights_loaded")
        s_weights_made = sem("s_weights_made")
        s_vec_constants = sem("s_vec_constants")
        s_ffn2_folded = sem("s_ffn2_folded")
        s_dft_w_copied = [sem(f"s_dft_w_copied{i}") for i in range(2)]
        s_idft_h_copied = [sem(f"s_idft_h_copied{i}") for i in range(2)]
        s_spec_copied = [sem(f"s_spec_copied{i}") for i in range(2)]
        s_rows_moved = [sem(f"s_rows_moved{i}") for i in range(4)]
        s_written = [sem(f"s_written{i}") for i in range(4)]
        s_x_loaded = [sem(f"s_x_loaded{i}") for i in range(2)]
        s_spectrum_padded = [sem(f"s_spectrum_padded{i}") for i in range(3)]
        s_filtered_moved = [sem(f"s_filtered_moved{i}") for i in range(4)]
        s_early_moved = [sem(f"s_early_moved{i}") for i in range(2)]
        s_im_made = [sem(f"s_im_made{i}") for i in range(2)]
        s_re_made = [sem(f"s_re_made{i}") for i in range(2)]
        s_local_moved = [sem(f"s_local_moved{i}") for i in range(2)]

        def bank(b, n=512, off=0):
            return PS[:, b, off:off + n]

        lay3 = lambda a, n: a.rearrange("p (a b) -> p a b", b=n)

        def later(n, least=1):
            return not isinstance(n, int) or n >= least

        SUM_FIRST, SUM_THEN = (0,), (1, 2, 3)
        QKV_BANK = (2, 3, 0, 2)

        XFIRST = 2

        def a_pe(pe, im, k, u, live):
            qk, _, at, ff, nm, tr = live
            if qk:
                if isinstance(k, int) and k == 0:
                    pe.wait_ge(s_x_loaded[0], (im + 1) * (XFIRST * 32))
                if isinstance(k, int) and k == 2 * XFIRST:
                    pe.wait_ge(s_x_loaded[1], (im + 1) * ((NCH // 2 - XFIRST) * 32))
                if later(k):
                    pe.wait_ge(s_qkv_copied, im * (NCH * RPC) + RPC * k)
                pe.matmul(bank(0), CEN, XC[:, bass.ds(k * CH, CH)], start=True, stop=True).then_inc(s_centred1, 1)
            if ff:
                pe.wait_ge(s_attn_relu, im * NCH + k - 2)
                pe.matmul(bank(5), W1[:, :], Y0, start=True, stop=True).then_inc(s_ffn1_made, 1)
            if qk:
                pe.wait_ge(s_square1, im * NCH + k + 1)
                if ff and (not isinstance(k, int) or k >= 4):
                    pe.wait_ge(s_ln2, im * NCH + k - 3)
                pe.matmul(bank(1), ONE, SQ[0], start=True, stop=True).then_inc(s_var1, 1)
            if ff:
                kk = k - 3
                pe.wait_ge(s_ffn1_relu, im * NCH + kk + 1)
                if later(kk):
                    pe.wait_ge(s_scaled2, im * NCH + kk)
                pe.matmul(bank(6), W2[:, :], Y1, start=True, stop=True).then_inc(s_ffn2_centred, 1)
            if nm:
                pe.wait_ge(s_square3, im * NCH + k - 3)
                if qk:
                    pe.wait_ge(s_ln1, im * NCH + k + 1)
                else:
                    pe.wait_ge(s_ln2, im * NCH + k - 3)
                pe.matmul(bank(1), ONE, SQ[2], start=True, stop=True).then_inc(s_var3, 1)
            if tr:
                pe.wait_ge(s_normed3, im * NCH + k - 4)
                if ff:
                    pe.wait_ge(s_ffn1_relu, im * NCH + k - 2)
                for r in range(RPC):
                    i = pe.transpose(bank(5, W, r * W), XT[:, r * W:(r + 1) * W], IDN)
                i.then_inc(s_transposed, 1)

            def sum_values(rows):
                pvv = PV[u % 2].rearrange("p (m r c) -> p r m c", r=RPC, m=NH)
                for r in rows:
                    for m in range(NH // 2):
                        i = pe.matmul(bank(4, W, r * W), pvv[:, r, m], IDN, start=(r == 0 and m == 0),
                                      stop=(r == RPC - 1 and m == NH // 2 - 1), skip_group_check=True)
                return i
            if ff:
                kk = k - 3
                pe.wait_ge(s_square2, im * NCH + kk + 1)
                if nm:
                    pe.wait_ge(s_ln3, im * NCH + k - 3)
                else:
                    pe.wait_ge(s_ln1, im * NCH + k + 1)
                pe.matmul(bank(1), ONE, SQ[1], start=True, stop=True).then_inc(s_var2, 1)
            if at:
                pe.wait_ge(s_pv_halved, im * NCH + k - 1)
                if later(k - 2):
                    pe.wait_ge(s_attn_copied, im * NCH + k - 2)
                sum_values(SUM_FIRST)
            if qk:
                pe.wait_ge(s_normed1, im * NCH + k + 1)
                for r in range(RPC):
                    if r == RPC - 1:
                        pe.wait_ge(s_qkv_copied, im * (NCH * RPC) + RPC * k + 1)
                    pe.matmul(bank(QKV_BANK[r], 384), XN[u % 4][:, r * W:(r + 1) * W], WQ[:, :],
                              start=True, stop=True).then_inc(s_qkv_made, 1)
            if at:
                sum_values(SUM_THEN).then_inc(s_attn_summed, 1)
            if ff:
                kk = k - 3
                pe.wait_ge(s_layer0_out, im * NCH + kk + 1)
                if later(kk):
                    pe.wait_ge(s_scaled3, im * NCH + kk)
                pe.matmul(bank(7), CEN, XC[:, bass.ds(kk * CH, CH)], start=True, stop=True).then_inc(s_centred3, 1)
            if at:
                pe.wait_ge(s_attn_copied, im * NCH + k - 1)
                if tr:
                    pe.wait_ge(s_pixels_copied, im * NCH + k - 4)
                pe.matmul(bank(5), WO[:, :], OS, start=True, stop=False)
                pe.matmul(bank(5), IDN, XN[(u - 2) % 4], start=False, stop=True).then_inc(s_attn_projected, 1)

        def rstd(act, im, k, src, dst, var, last_read, ln, done):
            act.wait_ge(var, im * NCH + k + 1)
            if later(k):
                act.wait_ge(last_read, im * NCH + k)
            act.activation(dst, src, ACT.Ln, bias=vec_of("eps")).then_inc(ln, 1)
            act.wait_ge(ln, im * NCH + k + 1)
            act.activation(dst, dst, ACT.Exp, scale=-0.5).then_inc(done, 1)

        def a_act(act, im, k, u, live):
            qk, sm, at, ff, nm, tr = live
            if qk:
                act.wait_ge(s_centred1, im * NCH + k + 1)
                act.activation(SQ[0], bank(0), ACT.Square).then_inc(s_square1, 1)
            if ff:
                act.wait_ge(s_ffn1_made, im * NCH + k - 2)
                act.activation(Y1, bank(5), ACT.Relu, bias=vec_of("f1b")).then_inc(s_ffn1_relu, 1)
            if qk:
                rstd(act, im, k, bank(1), RS[0], s_var1, s_scaled1, s_ln1, s_rstd1)
            if ff:
                act.wait_ge(s_ffn2_centred, im * NCH + k - 2)
                act.activation(SQ[1], bank(6), ACT.Square, bias=vec_of("f2c")).then_inc(s_square2, 1)
            if nm:
                rstd(act, im, k - 4, bank(1), RS[2], s_var3, s_scaled3, s_ln3, s_rstd3)
            if tr:
                kk = k - 5
                act.wait_ge(s_transposed, im * NCH + kk + 1)
                dst = XP1.rearrange("p (s h c) -> p s h c", s=2, c=C)[:, :, bass.ds(kk * RPC, RPC), :]
                act.activation(dst, bank(5).rearrange("p (r s c) -> p s r c", r=RPC, s=2), ACT.Copy).then_inc(s_pixels_copied, 1)
            if qk:
                act.wait_ge(s_scaled1, im * NCH + k + 1)
                act.activation(XN[u % 4], XH[0], ACT.Identity, bias=vec_of("b1")).then_inc(s_normed1, 1)
            if sm:
                kk = k - 1
                act.wait_ge(s_scores_shifted, im * NCH + kk + 1)
                act.activation(EX, SC, ACT.Exp, scale=HD ** -0.5).then_inc(s_score_exp, 1)
            if ff:
                rstd(act, im, k - 3, bank(1), RS[1], s_var2, s_scaled2, s_ln2, s_rstd2)

            def take_qkv(rows):
                qsv = QS[u % 2].rearrange("p (j r c) -> p r j c", j=3, r=RPC)
                for r in rows:
                    act.wait_ge(s_qkv_made, im * (NCH * RPC) + RPC * k + r + 1)
                    act.activation(qsv[:, r], bank(QKV_BANK[r], 384).rearrange("p (j c) -> p j c", j=3),
                                   ACT.Copy).then_inc(s_qkv_copied, 1)
            if qk:
                if later(k, 2):
                    act.wait_ge(s_pv_products, im * NCH + k - 1)
                take_qkv(range(RPC))
            if nm:
                act.wait_ge(s_scaled3, im * NCH + k - 3)
                act.activation(XT, XH[2], ACT.Identity, bias=vec_of("n1b")).then_inc(s_normed3, 1)
            if ff:
                kk = k - 3
                act.wait_ge(s_residual_added, im * NCH + kk + 1)
                act.activation(XC[:, bass.ds(kk * CH, CH)], XH[1], ACT.Relu, bias=vec_of("b2")).then_inc(s_layer0_out, 1)
            if at:
                act.wait_ge(s_attn_summed, im * NCH + k - 1)
                act.activation(OS, bank(4), ACT.Copy).then_inc(s_attn_copied, 1)
            if ff:
                act.wait_ge(s_centred3, im * NCH + k - 2)
                act.activation(SQ[2], bank(7), ACT.Square).then_inc(s_square3, 1)
            if at:
                act.wait_ge(s_attn_projected, im * NCH + k - 1)
                act.activation(Y0, bank(5), ACT.Relu).then_inc(s_attn_relu, 1)

        def a_dve(dve, im, k, u, live):
            qk, sm, _, ff, nm, _ = live
            if sm:
                kk = k - 1
                sc = lay3(SC, NH)
                dve.wait_ge(s_qk_products, im * NCH + kk + 1)
                if later(kk):
                    dve.wait_ge(s_score_exp, im * NCH + kk)
                dve.tensor_reduce(SC, lay3(PROD, HD), X, ALU.add).then_inc(s_scores, 1)
            if qk:
                dve.wait_ge(s_rstd1, im * NCH + k + 1)
                if later(k):
                    dve.wait_ge(s_normed1, im * NCH + k)
                dve.scalar_tensor_tensor(out=XH[0], in0=bank(0), scalar=vec_of("g1"), in1=RS[0],
                                         op0=ALU.mult, op1=ALU.mult).then_inc(s_scaled1, 1)
            if sm:
                kk = k - 1
                dve.wait_ge(s_scores, im * NCH + kk + 1)
                dve.tensor_reduce(MX, sc, X, ALU.max).then_inc(s_score_max, 1)
                dve.wait_ge(s_score_max, im * NCH + kk + 1)
                dve.tensor_tensor(sc, sc, MX.unsqueeze(2).broadcast_to([P, C, NH]), ALU.subtract).then_inc(s_scores_shifted, 1)
            if nm:
                kk = k - 4
                dve.wait_ge(s_rstd3, im * NCH + kk + 1)
                if later(kk):
                    dve.wait_ge(s_normed3, im * NCH + kk)
                dve.scalar_tensor_tensor(out=XH[2], in0=bank(7), scalar=vec_of("n1g"), in1=RS[2],
                                         op0=ALU.mult, op1=ALU.mult).then_inc(s_scaled3, 1)
            if sm:
                kk = k - 1
                ex = lay3(EX, NH)
                dve.wait_ge(s_score_exp, im * NCH + kk + 1)
                dve.tensor_reduce(SU, ex, X, ALU.add).then_inc(s_exp_sum, 1)
                dve.wait_ge(s_exp_sum, im * NCH + kk + 1)
                dve.reciprocal(RI, SU).then_inc(s_exp_sum_inv, 1)
                dve.wait_ge(s_exp_sum_inv, im * NCH + kk + 1)
                if later(kk):
                    dve.wait_ge(s_pv_products, im * NCH + kk)
                dve.tensor_tensor(lay3(PB, NH), ex, RI.unsqueeze(2).broadcast_to([P, C, NH]), ALU.mult).then_inc(s_probs, 1)
            if ff:
                kk = k - 3
                dve.wait_ge(s_rstd2, im * NCH + kk + 1)
                if later(kk):
                    dve.wait_ge(s_layer0_out, im * NCH + kk)
                dve.scalar_tensor_tensor(out=XH[1], in0=bank(6), scalar=vec_of("f2c"), in1=RS[1],
                                         op0=ALU.add, op1=ALU.mult).then_inc(s_scaled2, 1)
                dve.wait_ge(s_scaled2, im * NCH + kk + 1)
                dve.scalar_tensor_tensor(out=XH[1], in0=XH[1], scalar=vec_of("g2"), in1=XC[:, bass.ds(kk * CH, CH)],
                                         op0=ALU.mult, op1=ALU.add).then_inc(s_residual_added, 1)
            if qk:
                q = QS[u % 2].rearrange("p (j g n d) -> p j g n d", j=3, g=2 * RPC, n=NH)
                dve.wait_ge(s_qkv_copied, im * (NCH * RPC) + RPC * (k + 1))
                if later(k):
                    dve.wait_ge(s_scores, im * NCH + k)
                pr = PROD.rearrange("p (g n m d) -> p g n m d", g=2 * RPC, n=NH, m=NH)
                shape = [P, 2 * RPC, NH, NH, HD]
                dve.tensor_tensor(pr, q[:, 0].unsqueeze(3).broadcast_to(shape),
                                  q[:, 1].unsqueeze(2).broadcast_to(shape), ALU.mult).then_inc(s_qk_products, 1)

        def a_pool(pool, im, k, u, live):
            if live[1]:
                kk = k - 1
                pool.wait_ge(s_probs, im * NCH + kk + 1)
                if later(kk, 2):
                    pool.wait_ge(s_attn_summed, im * NCH + kk - 1)
                v = QS[(u - 1) % 2].rearrange("p (j r s m d) -> p j r s m d", j=3, r=RPC, s=2, m=NH)[:, 2]
                pb = PB.rearrange("p (r s n m) -> p r s n m", r=RPC, s=2, n=NH)
                tile_ = PV[(u - 1) % 2]
                pv = tile_.rearrange("p (m r s n d) -> p r s n m d", r=RPC, m=NH, s=2, n=NH)
                shape = [P, 2, NH, NH, HD]
                for r in range(RPC):
                    i = pool.tensor_tensor(pv[:, r], pb[:, r].unsqueeze(4).broadcast_to(shape),
                                           v[:, r].unsqueeze(2).broadcast_to(shape), ALU.mult)
                i.then_inc(s_pv_products, 1)
                pool.wait_ge(s_pv_products, im * NCH + kk + 1)
                n = NH // 2 * CH
                pool.tensor_tensor(tile_[:, 0:n], tile_[:, 0:n], tile_[:, n:2 * n], ALU.add).then_inc(s_pv_halved, 1)

        def pipeline(eng, stage, im):
            live = lambda k: tuple(0 <= k - j < NCH for j in range(6))
            for k in range(8):
                stage(eng, im, k, k % 4, live(k))
            with eng.Fori(2, NCH // 4) as k4:
                for u in range(4):
                    stage(eng, im, k4 * 4 + u, u, (True,) * 6)
            for k in range(NCH, NCH + 5):
                stage(eng, im, k, k % 4, live(k))

        B1 = [(i, min(3, C - i)) for i in range(0, C, 3)]
        B2 = [(i, min(4, KG - i)) for i in range(0, KG, 4)]
        NB1, NB2 = len(B1), len(B2)
        ENDS = (NB2 // 2, NB2 - 2, NB2)
        NP = len(ENDS)
        PIECES = [(B2[a][0], sum(n for _, n in B2[a:b])) for a, b in zip((0,) + ENDS, ENDS)]
        af = AF.rearrange("p (r k m) -> p r k m", r=2, k=KG)
        afc = AF.rearrange("p (r k g c) -> p r k g c", r=2, k=KG, g=2)

        def piece(a, p):
            return a[:, PIECES[p][0] * H:(PIECES[p][0] + PIECES[p][1]) * H]

        def b_pe(pe, im):
            pe.wait_ge(s_pixels_copied, (im + 1) * NCH)
            xp = XP1.rearrange("p (h c) -> p h c", c=C)
            for g, (c0, n) in enumerate(B1):
                if g >= 4:
                    pe.wait_ge(s_dft_w_copied[g % 2], im * (NB1 // 2) + (g - 4) // 2 + 1)
                for j in range(n):
                    i = pe.matmul(bank(g % 4, 130, j * 130), xp[:, :, c0 + j], DFTW, start=(j == 0),
                                  stop=(j == n - 1), skip_group_check=True)
                i.then_inc(s_dft_w_made, 1)
            pe.wait_ge(s_dft_w_copied[0], (im + 1) * (NB1 // 2))
            pe.wait_ge(s_dft_w_copied[1], (im + 1) * (NB1 // 2))
            for g, (k0, n) in enumerate(B2):
                if g >= 4:
                    pe.wait_ge(s_re_copied, im * NB2 + g - 3)
                    pe.wait_ge(s_im_copied, im * NB2 + g - 3)
                for j in range(n):
                    a, b = af[:, 0, k0 + j], af[:, 1, k0 + j]
                    for ri in range(2):
                        dst = bank(2 * (g % 4) + ri, H, j * H)
                        pe.matmul(dst, a, DRE[:, ri * H:(ri + 1) * H], start=(j == 0), stop=False,
                                  skip_group_check=True)
                        i = pe.matmul(dst, b, DIM[:, ri * H:(ri + 1) * H], start=False, stop=(j == n - 1),
                                      skip_group_check=True)
                i.then_inc(s_dft_h_made, 1)

        def b1_evac(eng, im, me, copy):
            for g, (c0, n) in enumerate(B1):
                if g % 2 == me:
                    eng.wait_ge(s_dft_w_made, im * NB1 + g + 1)
                    src = bank(g % 4, n * 130).rearrange("p (c r k) -> p r k c", c=n, r=2)
                    for h in range(2):
                        i = copy(afc[:, :, :, h, c0:c0 + n], src[:, :, 32 * h:32 * h + KG])
                    i.then_inc(s_dft_w_copied[me], 1)

        def b_act(act, im):
            b1_evac(act, im, 0, lambda o_, i_: act.activation(o_, i_, ACT.Copy))

            def power(dst, src, p, expo, bias, ready, ln, done):
                act.wait_ge(ready, im * NP + p + 1)
                act.activation(piece(dst, p), piece(src, p), ACT.Ln, bias=vec_of(bias)).then_inc(ln, 1)
                act.wait_ge(ln, im * NP + p + 1)
                act.activation(piece(dst, p), piece(dst, p), ACT.Exp, scale=expo).then_inc(done, 1)

            def magnitude(p):
                power(MG, MG, p, 0.5, "tiny", s_mag_squared, s_mag_ln, s_mag)

            def absolute(p):
                act.wait_ge(s_mag_squared, im * NP + p + 1)
                act.activation(piece(TT, p), piece(IM, p), ACT.Abs).then_inc(s_im_abs, 1)

            def inverse(p):
                power(TT, TT, p, -1.0, "tiny", s_phase_den, s_phase_den_ln, s_phase_den_inv)
            def re_square(p):
                act.wait_ge(s_re_copied, im * NB2 + ENDS[p])
                act.activation(piece(MG, p), piece(RE, p), ACT.Square).then_inc(s_re_square, 1)
            for g, (k0, n) in enumerate(B2):
                act.wait_ge(s_dft_h_made, im * NB2 + g + 1)
                act.activation(RE[:, k0 * H:(k0 + n) * H], bank(2 * (g % 4), n * H), ACT.Copy).then_inc(s_re_copied, 1)
                if g == ENDS[0] - 1:
                    re_square(0)
                elif g == ENDS[0]:
                    absolute(0)
                    magnitude(0)
                elif g == ENDS[1] - 1:
                    re_square(1)
                    inverse(0)
                elif g == ENDS[1]:
                    absolute(1)
                    magnitude(1)
            re_square(2)
            act.wait_ge(s_im_copied, (im + 1) * NB2)
            act.activation(piece(TT, 2), piece(IM, 2), ACT.Square).then_inc(s_im_square_last, 1)
            absolute(2)
            magnitude(2)
            inverse(1)
            inverse(2)
            for p in range(NP):
                act.wait_ge(s_half_tan, im * NP + p + 1)
                act.activation(piece(RE, p), piece(RE, p), ACT.Arctan).then_inc(s_half_angle, 1)

        def b_dve(dve, im):
            b1_evac(dve, im, 1, lambda o_, i_: dve.tensor_copy(o_, i_))
            def sums(p):
                dve.wait_ge(s_re_square, im * NP + p + 1)
                if p < NP - 1:
                    dve.wait_ge(s_im_square, im * (NP - 1) + p + 1)
                else:
                    dve.wait_ge(s_im_square_last, im + 1)
                dve.tensor_tensor(piece(MG, p), piece(MG, p), piece(TT, p), ALU.add).then_inc(s_mag_squared, 1)

            def denominator(p):
                dve.wait_ge(s_im_abs, im * NP + p + 1)
                dve.tensor_scalar(piece(IM, p), piece(IM, p), 0.0, 0.5, ALU.is_ge, ALU.subtract).then_inc(s_im_sign, 1)
                dve.wait_ge(s_mag, im * NP + p + 1)
                dve.tensor_tensor(piece(TT, p), piece(TT, p), piece(MG, p), ALU.add).then_inc(s_phase_den, 1)

            def half_tan(p):
                dve.wait_ge(s_phase_den_inv, im * NP + p + 1)
                dve.scalar_tensor_tensor(out=piece(RE, p), in0=piece(RE, p), scalar=TINY, in1=piece(TT, p),
                                         op0=ALU.add, op1=ALU.mult).then_inc(s_half_tan, 1)
            for g, (k0, n) in enumerate(B2):
                dve.wait_ge(s_dft_h_made, im * NB2 + g + 1)
                dve.tensor_copy(IM[:, k0 * H:(k0 + n) * H], bank(2 * (g % 4) + 1, n * H)).then_inc(s_im_copied, 1)
                if g == ENDS[0]:
                    sums(0)
                elif g == ENDS[1] - 1:
                    denominator(0)
                elif g == ENDS[1]:
                    sums(1)
                    half_tan(0)
            sums(2)
            denominator(1)
            denominator(2)
            half_tan(1)
            half_tan(2)
            dve.wait_ge(s_dft_h_made, (im + 1) * NB2)
            dve.memset(mp[:, 0:KX + 2:KX + 1, :], 0.0).then_inc(s_borders_zeroed, 1)
            dve.memset(mp[:, 1:KX + 1, 0:MPW:MPW - 1], 0.0).then_inc(s_borders_zeroed, 1)
            dve.memset(lp[:, 0:KX + 2:KX + 1, :], 0.0).then_inc(s_borders_zeroed, 1)
            for p in range(NP):
                dve.wait_ge(s_half_angle, im * NP + p + 1)
                dve.wait_ge(s_im_factor, im * NP + p + 1)
                dve.scalar_tensor_tensor(out=piece(RE, p), in0=piece(RE, p), scalar=0.5 * HALF_PI, in1=piece(IM, p),
                                         op0=ALU.subtract, op1=ALU.mult).then_inc(s_phase_done, 1)

        def b_pool(pool, im):
            whole = lambda name, p: vec_of(name).broadcast_to([P, PIECES[p][1] * H])
            for p in range(NP - 1):
                pool.wait_ge(s_im_copied, im * NB2 + ENDS[p])
                pool.tensor_tensor(piece(TT, p), piece(IM, p), piece(IM, p), ALU.mult).then_inc(s_im_square, 1)
            for p in range(NP):
                pool.wait_ge(s_phase_den, im * NP + p + 1)
                pool.tensor_tensor(piece(MG, p), piece(MG, p), whole("tiny_mag", p), ALU.add).then_inc(s_mag_done, 1)
                pool.wait_ge(s_im_sign, im * NP + p + 1)
                pool.tensor_tensor(piece(IM, p), piece(IM, p), whole("minus4", p), ALU.mult).then_inc(s_im_factor, 1)

        mp = MP.rearrange("p (k y) -> p k y", y=MPW)
        lp = LP.rearrange("p (k y) -> p k y", y=LPW)
        xpv = XP.rearrange("p (r c) -> p r c", c=XPW)

        def b_sync(sp, im):
            sp.wait_ge(s_dft_h_made, (im + 1) * NB2)
            for lo, src in ((0, MG), (C, RE)):
                for p, (k0, n) in enumerate(PIECES):
                    if src is RE:
                        sp.wait_ge(s_phase_done, im * NP + p + 1)
                    else:
                        sp.wait_ge(s_mag_done, im * NP + p + 1)
                    v = lay3(src, H)
                    k1 = max(k0, 1)
                    sp.dma_start(mp[lo:lo + C, 1 + k0:1 + k0 + n, 1:1 + H], v[0:C, k0:k0 + n]).then_inc(s_spectrum_padded[p], 16)
                    sp.dma_start(mp[lo:lo + C, 33 + k1:33 + k0 + n, 1:1 + H], v[C:P, k1:k0 + n]).then_inc(s_spectrum_padded[p], 16)

        C1R = 13
        NC1 = KX // C1R

        def c_pe(pe, im):
            pe.wait_ge(s_borders_zeroed, (im + 1) * 3)
            for g in range(NC1):
                if g < NP:
                    pe.wait_ge(s_spectrum_padded[g], (im + 1) * 64)
                if g >= 2:
                    pe.wait_ge(s_local_copied, im * NC1 + g - 1)
                for q in range(NQ):
                    i = pe.matmul(bank(g % 2, C1R * LPW), LW[:, q * P:(q + 1) * P],
                                  mp[:, 1 + g * C1R:1 + (g + 1) * C1R, q * QY:q * QY + LPW],
                                  start=(q == 0), stop=(q == NQ - 1))
                i.then_inc(s_local_made, 1)
            pe.wait_ge(s_local_sum, im + 1)
            pe.matmul(bank(2, 1), GC[:, :], SM[:, 0:1], start=True, stop=True).then_inc(s_gate_logit, 1)

        CUT = [0] + [C1R * (g + 1) - 1 for g in range(NC1 - 1)] + [KX]
        FIRST = 3

        def cut(a, g):
            return a[:, CUT[g] * QY:CUT[g + 1] * QY]

        HELPED = (6, 7, 8)
        N_DVE = T9 - len(HELPED)

        def dw_src(g, t):
            return lp[:, CUT[g] + t % 3:CUT[g + 1] + t % 3, t // 3:t // 3 + QY]

        def dw_count(im, g, n=None):
            each = T9 + (NC1 - 1) * N_DVE
            if g == 0:
                return im * each + (T9 if n is None else n)
            return im * each + T9 + (g - 1) * N_DVE + (N_DVE if n is None else n)

        def c_act(act, im):
            load_set(act, SET_SIGMOID)
            a_taps = lambda a, g: a[:, 0:(CUT[g + 1] - CUT[g]) * QY]
            for g in range(NC1 + 1):
                if g < NC1:
                    act.wait_ge(s_local_made, im * NC1 + g + 1)
                    act.activation(lp[:, 1 + g * C1R:1 + (g + 1) * C1R], lay3(bank(g % 2, C1R * LPW), LPW),
                                   ACT.Copy).then_inc(s_local_copied, 1)
                if 1 <= g < NC1:
                    if g >= 3:
                        act.wait_ge(s_dw_taps, dw_count(im, g - 2))
                    act.wait_ge(s_local_copied, im * NC1 + g + 1)
                    for j, t in enumerate(HELPED):
                        i = act.activation(lay3(a_taps(AT[g % 2][j], g), QY), dw_src(g, t), ACT.Copy, scale=DW[:, t:t + 1])
                    i.then_inc(s_act_taps, 1)
                if g >= 1:
                    act.wait_ge(s_dw_taps, dw_count(im, g - 1))
                    act.activation(cut(UU, g - 1), cut(AC, g - 1), ACT.Relu, bias=vec_of("three")).then_inc(s_local_relu3, 1)
            act.wait_ge(s_gate_logit, im + 1)
            act.activation(SM[:, 1:2], bank(2, 1), ACT.Sigmoid, bias=vec_of("gcb"),
                           scale=1.0 / (6 * KX * H)).then_inc(s_gate, 1)
            act.wait_ge(s_gate_factor, im + 1)
            act.activation(HWG, HW[:, :], ACT.Copy, scale=GMUL).then_inc(s_head_part1, 1)

        def c_dve(dve, im):
            dve.wait_ge(s_borders_zeroed, (im + 1) * 3)
            a3 = lay3(AC, QY)

            def swish(g):
                dve.wait_ge(s_local_relu3, im * NC1 + g + 1)
                dve.scalar_tensor_tensor(out=cut(AC, g), in0=cut(UU, g), scalar=6.0, in1=cut(AC, g), op0=ALU.min,
                                         op1=ALU.mult, accum_out=LSUM[:, g:g + 1]).then_inc(s_local_swish, 1)
            for g in range(NC1):
                dve.wait_ge(s_local_copied, im * NC1 + g + 1)
                out_ = a3[:, CUT[g]:CUT[g + 1]]
                for t in range(T9 if g == 0 else N_DVE):
                    w = DW[:, t:t + 1]
                    if t == 0 and g == 0:
                        dve.tensor_scalar(out_, dw_src(g, t), w, None, ALU.mult).then_inc(s_dw_taps, 1)
                        continue
                    if t == 0:
                        dve.wait_ge(s_taps_summed, im * (NC1 - 1) + g)
                        acc = lay3(AT[g % 2][0][:, 0:(CUT[g + 1] - CUT[g]) * QY], QY)
                    else:
                        dve.wait_ge(s_dw_taps, dw_count(im, g, t))
                        acc = out_
                    dve.scalar_tensor_tensor(out=out_, in0=dw_src(g, t), scalar=w, in1=acc, op0=ALU.mult,
                                             op1=ALU.add).then_inc(s_dw_taps, 1)
                if g >= 1:
                    swish(g - 1)
            swish(NC1 - 1)
            dve.wait_ge(s_local_swish, (im + 1) * NC1)
            dve.tensor_reduce(SM[:, 0:1], LSUM, X, ALU.add).then_inc(s_local_sum, 1)
            dve.wait_ge(s_gate, im + 1)
            dve.tensor_scalar(GMUL, SM[:, 1:2], vec_of("gate_mul"), vec_of("gate_add"), ALU.mult,
                              ALU.add).then_inc(s_gate_factor, 1)
            dve.wait_ge(s_head_part1, im + 1)
            r = slice(HEAD_W2H1, HEAD_W2H1 + FG)
            dve.scalar_tensor_tensor(out=HWG[r], in0=HW[r, :], scalar=SM[r, 45:46], in1=HWG[r],
                                     op0=ALU.mult, op1=ALU.subtract).then_inc(s_head_gated, 1)

        def c_pool(pool, im):
            for g in range(1, NC1):
                pool.wait_ge(s_act_taps, im * (NC1 - 1) + g)
                n = (CUT[g + 1] - CUT[g]) * QY
                a, b, c = (t[:, 0:n] for t in AT[g % 2])
                pool.tensor_tensor(a, a, b, ALU.add).then_inc(s_taps_paired, 1)
                pool.wait_ge(s_taps_paired, im * (NC1 - 1) + g)
                pool.tensor_tensor(a, a, c, ALU.add).then_inc(s_taps_summed, 1)

        MOVES = (3 * NQ * 16 + 16, 3 * NQ * 16)

        def c_sync(sp, im):
            loc = LOC.rearrange("p (q k) -> p q k", q=NQ)
            for half, (g0, g1) in enumerate(((0, FIRST), (FIRST, NC1))):
                sp.wait_ge(s_local_swish, im * NC1 + g1)
                cols = slice(CUT[g0] * QY, CUT[g1] * QY)
                for q in range(NQ):
                    for row in HEAD_GROUPS:
                        sp.dma_start(loc[row:row + FG, q, cols],
                                     AC[q * FG:(q + 1) * FG, cols]).then_inc(s_local_moved[half], 16)
                if half == 0:
                    sp.dma_start(LOC[HEAD_B1:HEAD_B2 + 1, :], ones).then_inc(s_local_moved[0], 16)

        NF = NQ * NK

        def at(n_g, n_q, lag, full):
            if not full and not 0 <= n_g * NQ + n_q - lag < NF:
                return None
            g, q = n_g + (n_q - lag) // NQ, (n_q - lag) % NQ
            return g, q, g * NQ + q

        def logits(q):
            return PS[:, 3 * (q % 2):3 * (q % 2) + 3, 0:3 * FN].rearrange("p b (t n) -> p b t n", t=3)

        def head_in(g, q):
            return LOC.rearrange("p (q k) -> p q k", q=NQ)[:, q, bass.ds(g * FN, FN)]

        def d_pe(pe, im, g0, q0, full):
            if now := at(g0, q0, 1, full):
                _, q, n = now
                b = 3 * (q % 2)
                pe.wait_ge(s_head_in_made, im * NF + n + 1)
                if later(n, 2):
                    pe.wait_ge(s_filt_exp, im * NF + n - 1)
                for t in range(T9):
                    i = pe.matmul(bank(b + t // 3, FN, (t % 3) * FN), HWG[:, t * P:(t + 1) * P], LOCP[q],
                                  start=(t % 3 == 0), stop=(t % 3 == 2), skip_group_check=True)
                i.then_inc(s_filt_logits, 1)
            if old := at(g0, q0, 4, full):
                _, qo, m = old
                pe.wait_ge(s_filt_products, im * NF + m + 1)
                if later(m, 2):
                    pe.wait_ge(s_filtered, im * NF + m - 1)
                for t in range(T9):
                    i = pe.matmul(bank(6 + qo % 2, FN), IDN, PD[qo][:, t * FN:(t + 1) * FN],
                                  start=(t == 0), stop=(t == T9 - 1))
                i.then_inc(s_filt_weighted, 1)
            if now:
                pe.wait_ge(s_filt_max, im * NF + n + 1)
                mx = MXF[q % 2].unsqueeze(1).broadcast_to([P, 3, FN])
                for j in range(3):
                    i = pe.matmul(bank(b + j, 3 * FN), NEGI[:, :], mx, start=False, stop=True,
                                  skip_group_check=True)
                i.then_inc(s_filt_shifted, 1)

        def d_dve(dve, im, g0, q0, full):
            if now := at(g0, q0, 1, full):
                _, q, n = now
                dve.wait_ge(s_filt_logits, im * NF + n + 1)
                if later(n, 2):
                    dve.wait_ge(s_filt_shifted, im * NF + n - 1)
                dve.tensor_reduce(MXF[q % 2], logits(q).rearrange("p b t n -> p n b t"),
                                  mybir.AxisListType.XY, ALU.max).then_inc(s_filt_max, 1)
            if nxt := at(g0, q0, 0, full):
                g, q, n = nxt
                r = slice(HEAD_W1H2, HEAD_W1H2 + FG)
                if isinstance(n, int) and n == 2 * NQ - 1:
                    dve.wait_ge(s_local_moved[1], (im + 1) * MOVES[1])
                dve.wait_ge(s_head_in_part1, im * NF + n + 1)
                dve.tensor_tensor(LOCP[q][r], head_in(g, q)[r], LOCP[q][r], ALU.subtract).then_inc(s_head_in_made, 1)
            if last := at(g0, q0, 2, full):
                _, q, n = last
                dve.wait_ge(s_filt_exp, im * NF + n + 1)
                if later(n, 2):
                    dve.wait_ge(s_filt_sum_inv, im * NF + n - 1)
                dve.tensor_reduce(DEN[q % 2], EE[q % 2].rearrange("p (t n) -> p n t", t=T9), X, ALU.add).then_inc(s_filt_sum, 1)
            if old := at(g0, q0, 4, full):
                g, q, n = old
                dve.wait_ge(s_filt_weighted, im * NF + n + 1)
                dve.wait_ge(s_filt_sum_inv, im * NF + n + 1)
                dst = lay3(FMP, H)[:, bass.ds(g * KR, KR), q * QY:(q + 1) * QY]
                dve.tensor_tensor(dst, lay3(bank(6 + q % 2, FN), QY), lay3(RDN[q], QY), ALU.mult).then_inc(s_filtered, 1)

        def d_act(act, im, g0, q0, full):
            if nxt := at(g0, q0, 0, full):
                g, q, n = nxt
                if isinstance(n, int) and n == 2 * NQ - 1:
                    act.wait_ge(s_local_moved[1], (im + 1) * MOVES[1])
                if later(n, 4):
                    act.wait_ge(s_filt_logits, im * NF + n - 3)
                act.activation(LOCP[q], head_in(g, q), ACT.Copy).then_inc(s_head_in_part1, 1)
            if now := at(g0, q0, 1, full):
                _, q, n = now
                if isinstance(n, int) and n == 0:
                    load_set(act, SET_LN_EXP)
                act.wait_ge(s_filt_shifted, im * NF + n + 1)
                if later(n, 2):
                    act.wait_ge(s_filt_products, im * NF + n - 1)
                    act.wait_ge(s_filt_sum, im * NF + n - 1)
                act.activation(EE[q % 2].rearrange("p (b t n) -> p b t n", b=3, t=3), logits(q),
                               ACT.Exp).then_inc(s_filt_exp, 1)
            if last := at(g0, q0, 2, full):
                _, q, n = last
                act.wait_ge(s_filt_sum, im * NF + n + 1)
                if later(n, 4):
                    act.wait_ge(s_filtered, im * NF + n - 3)
                act.activation(RDN[q], DEN[q % 2], ACT.Ln).then_inc(s_filt_ln, 1)
                act.wait_ge(s_filt_ln, im * NF + n + 1)
                act.activation(RDN[q], RDN[q], ACT.Exp, scale=-1.0).then_inc(s_filt_sum_inv, 1)

        def d_pool(pool, im, g0, q0, full):
            if now := at(g0, q0, 1, full):
                g, q, n = now
                pool.wait_ge(s_filt_exp, im * NF + n + 1)
                if later(n, 4):
                    pool.wait_ge(s_filt_weighted, im * NF + n - 3)
                for i in range(3):
                    e = EE[q % 2].rearrange("p (i j k y) -> p i j k y", i=3, j=3, k=KR)[:, i]
                    d = PD[q].rearrange("p (i j k y) -> p i j k y", i=3, j=3, k=KR)[:, i]
                    win = mp[:, bass.ds(g * KR, KR), q * QY + i:q * QY + i + QY]
                    win = bass.AP(win.tensor, win.offset, [list(win.ap[0]), [MPW, 3]] + [list(a) for a in win.ap[1:]])
                    ins = pool.tensor_tensor(d, e, win, ALU.mult)
                ins.then_inc(s_filt_products, 1)

        def filter_loop(eng, stage, im):
            for g in range(2):
                for q in range(NQ):
                    stage(eng, im, g, q, False)
            with eng.Fori(2, NK) as g:
                for q in range(NQ):
                    stage(eng, im, g, q, True)
            for q in range(4):
                stage(eng, im, NK, q, False)

        TG = [(0, 1)] + [(k, min(4, 32 - k)) for k in range(1, 32, 4)] + [(32, 1)]
        NT = 2 * len(TG)
        GROUPS = [(real, k0, m) for real in (False, True) for k0, m in TG]
        BEFORE_COS = 4
        za, zb = (a.rearrange("p (c k) -> p c k", k=P) for a in (ZA, ZB))
        bfc = BF.rearrange("p (h s c) -> p s h c", h=H // 2, s=2)

        def dve_turn(n):
            return (n ^ 1) + 1

        HALVES = ((0, 17), (17, KG))

        def half(a, p):
            return a[:, HALVES[p][0] * H:HALVES[p][1] * H]

        def e_sync(sp, im):
            f = lay3(FMP, H)

            def move(src, dst, g, p, done):
                k0, k1 = HALVES[p]
                sp.dma_start(lay3(dst, H)[g * C:(g + 1) * C, k0:k1],
                             src[:, 32 * g + k0:32 * g + k1]).then_inc(done, 16)
            done_g = -(-KG // KR)
            sp.wait_ge(s_filtered, im * NF + NQ * done_g)
            for p in range(2):
                move(f[C:P], FP2, 0, p, s_early_moved[p])
            sp.wait_ge(s_filtered, (im + 1) * NF)
            for p in range(2):
                move(f[C:P], FP2, 1, p, s_filtered_moved[p])
            for p in range(2):
                for g in range(2):
                    move(f[0:C], FM2, g, p, s_filtered_moved[2 + p])

        def e_pe(pe, im):
            n = 0
            for made, src in ((s_im_made, SN), (s_re_made, CO)):
                for k0, m in TG:
                    for p in range(2):
                        if k0 == HALVES[p][0]:
                            pe.wait_ge(made[p], im + 1)
                    if n >= 4:
                        pe.wait_ge(s_spec_copied[0], im * NT + n - 3)
                        pe.wait_ge(s_spec_copied[1], im * NT + dve_turn(n - 4))
                    for j in range(m):
                        i = pe.transpose(bank(n % 4, P, j * P), src[:, (k0 + j) * H:(k0 + j + 1) * H], IDN)
                    i.then_inc(s_spec_transposed, 1)
                    n += 1
            pe.wait_ge(s_spec_copied[0], (im + 1) * NT)
            pe.wait_ge(s_spec_copied[1], (im + 1) * NT)
            for g in range(C // 4):
                if g >= 4:
                    pe.wait_ge(s_idft_h_copied[g % 2], im * (C // 8) + (g - 4) // 2 + 1)
                for j in range(4):
                    c = 4 * g + j
                    pe.matmul(bank(g % 4, H, j * H), za[:, c], ICS[:, 0:H], start=(j == 0), stop=False,
                              skip_group_check=True)
                    i = pe.matmul(bank(g % 4, H, j * H), zb[:, c], ICS[:, H:2 * H], start=False, stop=(j == 3),
                                  skip_group_check=True)
                i.then_inc(s_idft_h_made, 1)
            pe.wait_ge(s_idft_h_copied[0], (im + 1) * (C // 8))
            pe.wait_ge(s_idft_h_copied[1], (im + 1) * (C // 8))
            for k in range(NCH):
                if k >= 4:
                    pe.wait_ge(s_x2_done, im * NCH + k - 3)
                for r in range(RPC):
                    h = RPC * k + r
                    i = pe.matmul(bank(k % 4, W, r * W), BF[:, h * P:(h + 1) * P], IFW,
                                  start=(r == 0), stop=(r == RPC - 1), skip_group_check=True)
                i.then_inc(s_idft_w_made, 1)

        def e_zcopy(im, me, eng, n, real, k0, m, emit):
            src = bank(n % 4, m * P).rearrange("p (t g c) -> p g c t", t=m, g=2)
            first = (real and me == 0) or (not real and me == 1)
            off = k0 if first else 64 + k0
            dst = (za, zb)[me]
            if first or 0 < k0 < 32:
                whole = dst[:, :, off:off + m]
                whole = bass.AP(whole.tensor, whole.offset, [list(whole.ap[0]), [32, 2]] + [list(a) for a in whole.ap[1:]])
                i = emit(whole, src, real)
            else:
                g = 1 if k0 == 0 else 0
                i = emit(dst[:, :, off + 32 * g:off + 32 * g + m], src[:, g], real)
            i.then_inc(s_spec_copied[me], 1)

        def e_act(act, im):
            for p in range(2):
                act.wait_ge(s_angle_clamped, im * 2 + p + 1)
                act.activation(half(SN, p), half(FP2, p), ACT.Sin).then_inc(s_sin_made, 1)

            def cosine(p):
                act.activation(half(CO, p), half(FP2, p), ACT.Abs).then_inc(s_angle_abs, 1)
                act.wait_ge(s_angle_abs, im * 2 + p + 1)
                act.activation(half(CO, p), half(CO, p), ACT.Sin, bias=vec_of("half_pi"), scale=-1.0).then_inc(s_cos_made, 1)
            cosine(0)
            for n, (real, k0, m) in enumerate(GROUPS):
                if n == BEFORE_COS:
                    cosine(1)
                act.wait_ge(s_spec_transposed, im * NT + n + 1)
                if n % 2:
                    act.wait_ge(s_spec_copied[1], im * NT + dve_turn(n))
                e_zcopy(im, 0, act, n, real, k0, m, lambda o_, i_, r_: act.activation(o_, i_, ACT.Copy))
            for g in range(0, C // 4, 2):
                act.wait_ge(s_idft_h_made, im * (C // 4) + g + 1)
                act.activation(bfc[:, :, :, 4 * g:4 * g + 4], bank(g % 4).rearrange("p (c s h) -> p s h c", c=4, s=2),
                               ACT.Copy).then_inc(s_idft_h_copied[0], 1)

        def e_dve(dve, im):
            for p in range(2):
                dve.wait_ge(s_early_moved[p], (im + 1) * 16)
                dve.wait_ge(s_filtered_moved[p], (im + 1) * 16)
                dve.tensor_scalar(half(FP2, p), half(FP2, p), PI, -PI, ALU.min, ALU.max).then_inc(s_angle_clamped, 1)
            for p in range(2):
                dve.wait_ge(s_sin_made, im * 2 + p + 1)
                dve.wait_ge(s_filtered_moved[2 + p], (im + 1) * 32)
                dve.tensor_tensor(half(SN, p), half(SN, p), half(FM2, p), ALU.mult).then_inc(s_im_made[p], 1)
            for turn in range(NT):
                if turn == BEFORE_COS:
                    dve.wait_ge(s_cos_made, im * 2 + 1)
                    dve.tensor_tensor(half(CO, 0), half(CO, 0), half(FM2, 0), ALU.mult).then_inc(s_re_made[0], 1)
                n = turn ^ 1
                real, k0, m = GROUPS[n]
                dve.wait_ge(s_spec_transposed, im * NT + n + 1)
                if n % 2 == 0:
                    dve.wait_ge(s_spec_copied[0], im * NT + n + 1)
                e_zcopy(im, 1, dve, n, real, k0, m,
                        lambda o_, i_, r_: dve.tensor_copy(o_, i_) if r_ else
                        dve.tensor_scalar(o_, i_, -1.0, None, ALU.mult))
            for g in range(1, C // 4, 2):
                dve.wait_ge(s_idft_h_made, im * (C // 4) + g + 1)
                dve.tensor_copy(bfc[:, :, :, 4 * g:4 * g + 4], bank(g % 4).rearrange("p (c s h) -> p s h c", c=4, s=2)).then_inc(s_idft_h_copied[1], 1)
            for k in range(NCH):
                dve.wait_ge(s_idft_w_made, im * NCH + k + 1)
                dve.tensor_tensor(XC[:, k * CH:(k + 1) * CH], XC[:, k * CH:(k + 1) * CH], bank(k % 4),
                                  ALU.add).then_inc(s_x2_done, 1)
            dve.memset(xpv[:, 0:H + 2:H + 1, :], 0.0).then_inc(s_image_borders_zeroed, 1)
            dve.memset(xpv[:, 1:H + 1, 0:XPW:XPW - 1], 0.0).then_inc(s_image_borders_zeroed, 1)

        def e_pool(pool, im):
            pool.wait_ge(s_cos_made, (im + 1) * 2)
            pool.wait_ge(s_filtered_moved[3], (im + 1) * 32)
            pool.tensor_tensor(half(CO, 1), half(CO, 1), half(FM2, 1), ALU.mult).then_inc(s_re_made[1], 1)

        def convs(k):
            if isinstance(k, int):
                first = [(max(2 * k - 7, 0), k - 3)] if 3 <= k <= NCH + 3 else []
                second = [(2 * k - 6, k + 13)] if 4 <= k <= NCH + 2 else []
                return first, second
            return [(k * 2 - 7, k - 3)], [(k * 2 - 6, k + 13)]

        def first_bank(m, u):
            return 0 if isinstance(m, int) and m == 0 else (2 * u - 7) % 4

        def f_pe(pe, im):
            def conv(m, mu, y):
                if later(m, 4):
                    pe.wait_ge(s_hidden_done, im * NY + m - 3)
                pe.wait_ge(s_rows_made, im * NY + m + 1)
                for t in range(T9):
                    src = lay3(XW[mu % 2], XPW)[:, t // 3:t // 3 + 4, t % 3:t % 3 + W]
                    for w in (CW2, CW1):
                        i = pe.matmul(bank(2 + mu % 4), w[:, t * P:(t + 1) * P], src,
                                      start=(t == 0 and w is CW2), stop=(t == T9 - 1 and w is CW1))
                i.then_inc(s_conv_made, 1)

            def step(k, u, rnd):
                norm = not isinstance(k, int) or k < NCH
                first, second = convs(k)
                if norm:
                    pe.wait_ge(s_x2_done, (im + 1) * NCH)
                    if later(k):
                        pe.wait_ge(s_scaled4, im * NCH + k)
                    pe.matmul(bank(0), CEN, XC[:, bass.ds(k * CH, CH)], start=True, stop=True).then_inc(s_centred4, 1)
                for m, y in first:
                    conv(m, first_bank(m, u), y)
                if norm:
                    pe.wait_ge(s_square4, im * NCH + k + 1)
                    pe.matmul(bank(1), ONE, SQE, start=True, stop=True).then_inc(s_var4, 1)
                for m, y in second:
                    conv(m, (2 * u - 6) % 4, y)
            for k in range(8):
                step(k, k % 4, k // 4)
            with pe.Fori(2, NCH // 4) as k4:
                for u in range(4):
                    step(k4 * 4 + u, u, k4)
            for k in range(NCH, NCH + 4):
                step(k, k % 4, k // 4)

            pe.wait_ge(s_hidden_sum, im + 1)
            pe.matmul(bank(6, 1)[0:FG], SE1[:, :], SM[:, 2:3], start=True, stop=True).then_inc(s_se1_made, 1)
            pe.wait_ge(s_se1_relu, im + 1)
            pe.matmul(bank(6, 1, 8), SE2[:, :], SM[0:FG, 3:4], start=True, stop=True).then_inc(s_se2_made, 1)
            pe.wait_ge(s_w_out_scaled, im + 1)

            def project(k, u):
                for h in range(2):
                    i = pe.matmul(bank(2 + u), WS[:, h * P:(h + 1) * P], HID[:, bass.ds(k * CH + h * (H * W // 2), CH)],
                                  start=(h == 0), stop=(h == 1))
                i.then_inc(s_projected, 1)
            for k in range(4):
                project(k, k)
            with pe.Fori(1, NCH // 4) as k4:
                for u in range(4):
                    pe.wait_ge(s_out_ready, im * NCH + k4 * 4 + u - 3)
                    project(k4 * 4 + u, u)

        def f_act(act, im):
            def relu3(m, mu):
                act.wait_ge(s_conv_made, im * NY + m + 1)
                if later(m, 2):
                    act.wait_ge(s_hidden_done, im * NY + m - 1)
                act.activation(UE[mu % 2], bank(2 + mu % 4), ACT.Relu, bias=vec_of("three")).then_inc(s_conv_relu3, 1)

            def part1(m, mu, y):
                if later(m, 2):
                    act.wait_ge(s_conv_made, im * NY + m - 1)
                act.activation(lay3(XW[mu % 2], XPW), xpv[:, bass.ds(y * 4, 6), :], ACT.Copy).then_inc(s_rows_part1, 1)

            def moved(k, u, rnd):
                r = rnd - 1 if u < 1 else rnd
                act.wait_ge(s_rows_moved[(u - 1) % 4], (im * (NCH // 4) + r + 1) * 64)

            def step(k, u, rnd):
                norm = not isinstance(k, int) or k < NCH
                first, second = convs(k)
                coming, _ = convs(k + 1)
                if norm:
                    act.wait_ge(s_centred4, im * NCH + k + 1)
                    act.activation(SQE, bank(0), ACT.Square).then_inc(s_square4, 1)
                for m, y in second:
                    part1(m, (2 * u - 6) % 4, y)
                for m, y in first:
                    relu3(m, first_bank(m, u))
                if norm:
                    act.wait_ge(s_var4, im * NCH + k + 1)
                    act.activation(RSE, bank(1), ACT.Ln, bias=vec_of("eps")).then_inc(s_ln4, 1)
                    act.wait_ge(s_ln4, im * NCH + k + 1)
                    act.activation(RSE, RSE, ACT.Exp, scale=-0.5).then_inc(s_rstd4, 1)
                    act.wait_ge(s_scaled4, im * NCH + k + 1)
                    act.activation(XNE[u % 2], XNE[u % 2], ACT.Identity, bias=vec_of("n2b")).then_inc(s_normed4, 1)
                if isinstance(k, int) and k == 2:
                    act.wait_ge(s_image_borders_zeroed, (im + 1) * 2)
                    moved(1, 1, 0)
                for m, y in coming:
                    if norm or k <= NCH:
                        moved(k, u, rnd)
                    part1(m, first_bank(m, (u + 1) % 4), y)
                for m, y in second:
                    relu3(m, (2 * u - 6) % 4)
            for k in range(8):
                step(k, k % 4, k // 4)
            with act.Fori(2, NCH // 4) as k4:
                for u in range(4):
                    step(k4 * 4 + u, u, k4)
            for k in range(NCH, NCH + 4):
                step(k, k % 4, k // 4)
            act.wait_ge(s_se1_made, im + 1)
            act.activation(SM[0:FG, 3:4], bank(6, 1)[0:FG], ACT.Relu, bias=vec_of("se1b", FG),
                           scale=1.0 / (6 * H * W)).then_inc(s_se1_relu, 1)
            act.wait_ge(s_se2_made, im + 1)
            act.activation(SM[:, 4:5], bank(6, 1, 8), ACT.Relu, bias=vec_of("se2b3")).then_inc(s_se2_relu, 1)

        def f_dve(dve, im):
            def swish(m, mu, y):
                dve.wait_ge(s_conv_relu3, im * NY + m + 1)
                dve.scalar_tensor_tensor(out=HID[:, bass.ds(y * CH, CH)], in0=UE[mu % 2], scalar=6.0,
                                         in1=bank(2 + mu % 4), op0=ALU.min, op1=ALU.mult,
                                         accum_out=SM[:, bass.ds(m + 8, 1)]).then_inc(s_hidden_done, 1)

            def part2(m, mu, y):
                hi = slice(C, P)
                dve.wait_ge(s_rows_part1, im * NY + m + 1)
                rows = lay3(XW[mu % 2], XPW)[hi]
                dve.tensor_tensor(rows, xpv[hi, bass.ds(y * 4, 6), :], rows, ALU.subtract).then_inc(s_rows_made, 1)

            def step(k, u, rnd):
                norm = not isinstance(k, int) or k < NCH
                first, second = convs(k)
                coming, _ = convs(k + 1)
                for m, y in second:
                    part2(m, (2 * u - 6) % 4, y)
                for m, y in first:
                    swish(m, first_bank(m, u), y)
                if norm:
                    dve.wait_ge(s_rstd4, im * NCH + k + 1)
                    if later(k, 2):
                        r = rnd - 1 if u < 2 else rnd
                        dve.wait_ge(s_rows_moved[(u - 2) % 4], (im * (NCH // 4) + r + 1) * 64)
                    dve.scalar_tensor_tensor(out=XNE[u % 2], in0=bank(0), scalar=vec_of("n2g"), in1=RSE, op0=ALU.mult,
                                             op1=ALU.mult).then_inc(s_scaled4, 1)
                for m, y in coming:
                    part2(m, first_bank(m, (u + 1) % 4), y)
                for m, y in second:
                    swish(m, (2 * u - 6) % 4, y)
            for k in range(8):
                step(k, k % 4, k // 4)
            with dve.Fori(2, NCH // 4) as k4:
                for u in range(4):
                    step(k4 * 4 + u, u, k4)
            for k in range(NCH, NCH + 4):
                step(k, k % 4, k // 4)
            dve.wait_ge(s_hidden_done, (im + 1) * NY)
            dve.tensor_reduce(SM[:, 2:3], SUMH, X, ALU.add).then_inc(s_hidden_sum, 1)
            dve.wait_ge(s_se2_relu, im + 1)
            dve.tensor_scalar(SM[:, 5:6], SM[:, 4:5], 6.0, 1.0 / 36, ALU.min, ALU.mult).then_inc(s_se_gate, 1)
            dve.wait_ge(s_se_gate, im + 1)
            dve.tensor_scalar(WS, WF[:, :], SM[:, 5:6], None, ALU.mult).then_inc(s_w_out_scaled, 1)

            def add_out(k, u, j=0):
                dve.wait_ge(s_projected, im * NCH + k + 1)
                if not isinstance(k, int):
                    dve.wait_ge(s_written[u], (im * (NCH // 4) + j) * 32)
                dve.scalar_tensor_tensor(out=OB[u], in0=bank(2 + u), scalar=vec_of("ob"),
                                         in1=XC[:, bass.ds(k * CH, CH)], op0=ALU.add, op1=ALU.add).then_inc(s_out_ready, 1)
            for k in range(4):
                add_out(k, k)
            with dve.Fori(1, NCH // 4) as k4:
                for u in range(4):
                    add_out(k4 * 4 + u, u, k4)

        def f_sync(sp, im, more):
            with sp.Fori(0, NCH // 4) as k4:
                for u in range(4):
                    k = k4 * 4 + u
                    sp.wait_ge(s_image_borders_zeroed, (im + 1) * 2)
                    sp.wait_ge(s_normed4, im * NCH + k + 1)
                    for h in range(2):
                        for to in range(2):
                            sp.dma_start(xpv[to * C:(to + 1) * C, bass.ds(k * RPC + h * (H // 2) + 1, RPC), 1:1 + W],
                                         lay3(XNE[u % 2][h * C:(h + 1) * C], W)).then_inc(s_rows_moved[u], 16)
            xo = out.rearrange("b c (s h) w -> b s c (h w)", s=2)
            def store(k, u):
                sp.wait_ge(s_out_ready, im * NCH + k + 1)
                for h in range(2):
                    sp.dma_start(xo[bass.ds(im, 1), h, :, bass.ds(k * CH, CH)].squeeze(0),
                                 OB[u][h * C:(h + 1) * C]).then_inc(s_written[u], 16)
            for u in range(4):
                store(u, u)
                if more and u % 2:
                    x_load(sp, im + 1, u // 2, 0)
            with sp.Fori(1, NCH // 4 - 1) as k4:
                for u in range(4):
                    store(k4 * 4 + u, u)
                    if more and u % 2:
                        x_load(sp, im + 1, k4 * 2 + u // 2, 1)
            for u in range(4):
                store(NCH - 4 + u, u)
            for u in range(4):
                sp.wait_ge(s_written[u], (im + 1) * (NCH * 8))
            if more:
                x_load(sp, im + 1, NCH // 2 - 2, 1)
                x_load(sp, im + 1, NCH // 2 - 1, 1)

        xi = x.rearrange("b c (s h) w -> b s c (h w)", s=2)

        def x_load(sp, im, j, group):
            for h in range(2):
                sp.dma_start(XC[h * C:(h + 1) * C, bass.ds(j * 2 * CH, 2 * CH)],
                             xi[bass.ds(im, 1), h, :, bass.ds(j * 2 * CH, 2 * CH)].squeeze(0)).then_inc(s_x_loaded[group], 16)

        def load_set(act, n):
            tables[0] += 1
            act.add_instruction(mybir.InstLoadActFuncSet(
                name=f"I-{900000 + tables[0]}", act_func_set_id=n, engine=mybir.EngineType.Activation,
                ins=[], outs=[]))
        tables = [0]

        def weight_loads():
            yield TB[:, :], tabs
            yield V[:, 0:NLOADED], vec
            wq = WQ[:, :].rearrange("p (j s c) -> p j s c", j=3, s=2)
            for h in range(2):
                r = slice(h * C, (h + 1) * C)
                yield wq[r, :, h], wqkv
                yield WO[r, r], wo
                yield W1[r, r], f1t
                yield WN[r, r], f2
                yield W1D[r, :], w1t
                yield WF[:, h * P + h * C:h * P + (h + 1) * C], w2t
            for q in range(NQ):
                yield LW[:, q * P + q * FG:q * P + (q + 1) * FG], l1t
                yield DW[q * FG:(q + 1) * FG, :], dwt
                for row in HEAD_GROUPS:
                    yield GC[q * FG:(q + 1) * FG, row:row + FG], gct
            for row in HEAD_GROUPS:
                yield HW[row:row + FG, :], head
            for row in (HEAD_B1, HEAD_B2):
                yield HW[row:row + 1, :], head_b
            yield D9[:, :], d9.partition_broadcast(P)
            yield SE1[:, :], se1t
            yield SE2[:, :], se2t
        N_W = len(list(weight_loads())) * 16

        block = ctx.enter_context(nc.Block())

        @block.sync
        def _(sp):
            sp.wait_ge(s_weights_zeroed, 8)
            for dst, src in weight_loads():
                sp.dma_start(dst, src).then_inc(s_weights_loaded, 16)
            sp.wait_ge(s_weights_made, 9)
            for j in range(XFIRST):
                x_load(sp, 0, j, 0)
            with sp.Fori(XFIRST, NCH // 2) as j:
                x_load(sp, 0, j, 1)

            def image(im, more):
                b_sync(sp, im)
                c_sync(sp, im)
                e_sync(sp, im)
                f_sync(sp, im, more)
            if n_img > 1:
                with sp.Fori(0, n_img - 1) as im:
                    image(im, True)
            image(n_img - 1, False)
            for u in range(4):
                sp.wait_ge(s_written[u], n_img * NCH * 8)

        @block.gpsimd
        def _(pool):
            for t in (WQ, WO, W1, LW, WF, HW, GC):
                pool.memset(t[:, :], 0.0).then_inc(s_weights_zeroed, 1)
            pool.memset(WN, 0.0).then_inc(s_weights_zeroed, 1)
            for i, v in enumerate((1e-5, HALF_PI, 3.0, 1e-8, TINY, -4.0)):
                pool.memset(V[:, NLOADED + i:NLOADED + i + 1], v).then_inc(s_vec_constants, 1)
            with pool.Fori(0, n_img) as im:
                pipeline(pool, a_pool, im)
                b_pool(pool, im)
                c_pool(pool, im)
                filter_loop(pool, d_pool, im)
                e_pool(pool, im)

        @block.tensor
        def _(pe):
            pe.wait_ge(s_weights_loaded, N_W)
            pe.matmul(bank(0, P), WN, CEN, start=True, stop=True)
            pe.matmul(bank(0, 1, P), CEN, vec_of("f2b"), start=True, stop=True).then_inc(s_ffn2_folded, 1)
            pe.wait_ge(s_weights_made, 9)
            with pe.Fori(0, n_img) as im:
                pipeline(pe, a_pe, im)
                b_pe(pe, im)
                c_pe(pe, im)
                pe.wait_ge(s_head_gated, im + 1)
                filter_loop(pe, d_pe, im)
                e_pe(pe, im)
                f_pe(pe, im)

        @block.scalar
        def _(act):
            act.wait_ge(s_weights_loaded, N_W)
            act.wait_ge(s_vec_constants, 6)
            act.wait_ge(s_weights_made, 9)
            with act.Fori(0, n_img) as im:
                load_set(act, SET_LN_EXP)
                pipeline(act, a_act, im)
                b_act(act, im)
                c_act(act, im)
                act.wait_ge(s_local_moved[0], (im + 1) * MOVES[0])
                filter_loop(act, d_act, im)
                e_act(act, im)
                load_set(act, SET_LN_EXP)
                f_act(act, im)

        @block.vector
        def _(dve):
            dve.wait_ge(s_weights_loaded, N_W)
            dve.wait_ge(s_vec_constants, 6)
            taps = lambda a: a.rearrange("p (t k) -> p t k", t=T9)
            dve.tensor_tensor(taps(W9), W1D.unsqueeze(1).broadcast_to([P, T9, P]), taps(D9), ALU.mult).then_inc(s_weights_made, 1)
            dve.wait_ge(s_weights_made, 1)
            dve.tensor_copy(CW1[:, :], W9).then_inc(s_weights_made, 1)
            dve.wait_ge(s_weights_made, 2)
            dve.tensor_tensor(CW2[:, :], W9, CW1[:, :], ALU.subtract).then_inc(s_weights_made, 1)
            dve.tensor_scalar(vec_of("se2b3"), vec_of("se2b"), 3.0, None, ALU.add).then_inc(s_weights_made, 1)
            dve.tensor_scalar(NEGI[:, :], IDN, -1.0, None, ALU.mult).then_inc(s_weights_made, 1)
            r = slice(HEAD_B1, HEAD_B1 + FG)
            dve.tensor_copy(PR[r, 0:T9 * P], HW[r, :]).then_inc(s_weights_made, 1)
            dve.wait_ge(s_weights_made, 5 + 1)
            dve.scalar_tensor_tensor(out=HW[r, :], in0=PR[r, 0:T9 * P], scalar=vec_of("minus_b2")[r], in1=HW[r, :],
                                     op0=ALU.mult, op1=ALU.add).then_inc(s_weights_made, 1)
            dve.wait_ge(s_ffn2_folded, 1)
            dve.tensor_copy(W2[:, :], bank(0, P)).then_inc(s_weights_made, 1)
            dve.tensor_copy(vec_of("f2c"), bank(0, 1, P)).then_inc(s_weights_made, 1)
            with dve.Fori(0, n_img) as im:
                pipeline(dve, a_dve, im)
                b_dve(dve, im)
                c_dve(dve, im)
                dve.wait_ge(s_local_moved[0], (im + 1) * MOVES[0])
                filter_loop(dve, d_dve, im)
                e_dve(dve, im)
                f_dve(dve, im)


def _tables():
    import numpy as np
    n = np.arange(P)
    blk = (n[:, None] // C == n[None, :] // C) / C
    k = np.arange(KX)

    def trig(a, b, f):
        m = np.outer(a, b) % P
        t = f(2 * np.pi * np.arange(P) / P)
        t[np.abs(t) < 1e-12] = 0
        return t[m]
    cw, sw = trig(n, k, np.cos), trig(n, k, np.sin)
    ch, sh = trig(n, n, np.cos), trig(n, n, np.sin)
    mult = np.where((k == 0) | (k == KX - 1), 1.0, 2.0)[:, None]
    inv = np.concatenate([mult * cw.T, (-2.0 * sw.T)[1:KX - 1]], 0) / P
    return np.concatenate([np.eye(P), np.eye(P) - blk, blk, cw / P, -sw / P, ch, -sh, sh, ch, ch, sh, inv],
                          1).astype(np.float32)


def kernel(**inputs):
    import numpy as np
    import concourse.bacc as bacc
    from concourse.bass_utils import run_bass_kernel_spmd

    a = {k: np.asarray(v) for k, v in inputs.items()}
    l0 = lambda n: a["L0_conv_" + n]
    l1 = lambda n: a["L1_conv_" + n]
    twice = lambda v: np.tile(v, 2)

    def head_rows(v):
        rows = np.zeros(P, v.dtype)
        for row in HEAD_GROUPS:
            rows[row:row + FG] = v
        return rows
    bias_rows = np.zeros(P, np.float32)
    bias_rows[[HEAD_B1, HEAD_B2]] = 1
    minus_b2 = np.zeros(P, np.float32)
    minus_b2[HEAD_B2] = -1
    vec = np.stack([twice(l0("g1")), twice(l0("b1")), twice(l0("ffn1_b")), twice(l0("ffn2_b")), twice(l0("g2")),
                    twice(l0("b2")), twice(l1("norm1_g")), twice(l1("norm1_b")), twice(l1("norm2_g")),
                    twice(l1("norm2_b")), twice(l1("ffn2_b")), head_rows(l1("fgn_gc_b")), l1("se2_b"),
                    np.tile(l1("se1_b"), NQ), head_rows(np.full(FG, 1 / 6, np.float32)), bias_rows, minus_b2], 1)
    arrays = {
        "x": a["x"],
        "vec": vec,
        "tabs": _tables(),
        "wqkv": np.stack([l0(n).reshape(C, C) for n in ("W_Q", "W_K", "W_V")], 1),
        "wo": l0("W_O"),
        "f1t": l0("ffn1_w").T,
        "f2": l0("ffn2_w"),
        "l1t": l1("fgn_l1_w").T,
        "dwt": l1("fgn_dw_w").reshape(FG, T9),
        "gct": l1("fgn_gc_w").T,
        "head": l1("fgn_head_w").reshape(2, C, T9, FG).transpose(3, 2, 0, 1).reshape(FG, T9 * P),
        "head_b": l1("fgn_head_b").reshape(2, C, T9).transpose(2, 0, 1).reshape(1, T9 * P),
        "w1t": l1("ffn1_w").T,
        "d9": l1("ffn_dw_w").reshape(P, T9).T.reshape(T9 * P),
        "se1t": l1("se1_w").T,
        "se2t": l1("se2_w").T,
        "w2t": l1("ffn2_w").T,
        "ones": np.ones((2, NQ * KX * QY), np.float32),
    }
    arrays = {k + "_dram": np.ascontiguousarray(v) for k, v in arrays.items()}
    nc = bacc.Bacc("TRN2", target_bir_lowering=False, num_devices=1)
    args = [nc.dram_tensor(k, v.shape, mybir.dt.from_np(v.dtype), kind="ExternalInput").ap() for k, v in arrays.items()]
    out = nc.dram_tensor("out_dram", a["x"].shape, F32, kind="ExternalOutput").ap()
    build(nc, *args, out)
    r = run_bass_kernel_spmd(nc, [arrays], core_ids=[0])
    return r.results[0]["out_dram"]
```
